# Optimizing a Trainium2 kernel written in Bass

```python
import numpy as np
import jax
import jax.numpy as jnp

def _softmax(x, axis=-1):
    return jax.nn.softmax(x, axis=axis)

def _gelu(x):
    return jax.nn.gelu(x, approximate=True)

def _silu(x):
    return jax.nn.silu(x)

def _sigmoid(x):
    return jax.nn.sigmoid(x)

def _layernorm(x, axis=-1, eps=1e-05):
    m = jnp.mean(x, axis=axis, keepdims=True)
    v = jnp.var(x, axis=axis, keepdims=True)
    return (x - m) / jnp.sqrt(v + eps)

def _scatter_add(tgt, idx, src, axis=0):
    return tgt.at[idx].add(src)

def _segment_sum(src, seg, n):
    return jax.ops.segment_sum(src, seg, n)
kernel_name = 'mk_lm_tower_d1_tok_ids1024_r4_27d7bc'

def setup_inputs(seed: int=0):
    np.random.seed(seed)
    _w = jnp.asarray

    def _rec_inputs():
        import jax
        import jax.numpy as jnp
        _rk = jax.random.key(seed)
        x = jax.random.randint(jax.random.fold_in(_rk, 1), (16, 512), 0, 127998, jnp.int32)
        return x
    x = _rec_inputs()

    def _L0_tok_setup():
        import jax, jax.numpy as jnp
        import numpy as np
        VOCAB = 32000
        D_EMBED = 256
        D_PROJ = 256
        DIV_VAL = 4
        CUTOFFS = [5000, 10000, 25000, VOCAB]
        CUT_ENDS = [0] + CUTOFFS
        key = jax.random.key(seed)
        ks = jax.random.split(key, 2 * len(CUTOFFS) + 1)
        inp = jax.random.randint(ks[0], (8, 512), 0, VOCAB, dtype=jnp.int64 if jax.config.jax_enable_x64 else jnp.int32)
        d = {'inp': inp}
        for i in range(len(CUTOFFS)):
            l, r = (CUT_ENDS[i], CUT_ENDS[i + 1])
            de = D_EMBED // DIV_VAL ** i
            d[f'emb_{i}'] = jax.random.normal(ks[2 * i + 1], (r - l, de), jnp.float32) * 0.02
            d[f'proj_{i}'] = jax.random.normal(ks[2 * i + 2], (D_PROJ, de), jnp.float32) * 0.02
        return d
    _L0_tok_all = _L0_tok_setup()
    _L0_tok_in = {k: v for k, v in _L0_tok_all.items() if k in ('emb_0', 'proj_0', 'emb_1', 'proj_1', 'emb_2', 'proj_2', 'emb_3', 'proj_3')}
    del _L0_tok_all

    def _L0_attn_setup():
        import jax, jax.numpy as jnp
        import numpy as np
        GROUP = 64
        MAX_REL = 32

        def _silu(x):
            return x * jax.nn.sigmoid(x)

        def _ln(x, w, b, eps=1e-05):
            m = x.mean(-1, keepdims=True)
            v = ((x - m) ** 2).mean(-1, keepdims=True)
            return (x - m) / jnp.sqrt(v + eps) * w + b

        def _rope(x):
            n, d = (x.shape[-2], x.shape[-1])
            half = d // 2
            pos = jnp.arange(n, dtype=x.dtype)
            inv_freq = 10000.0 ** (-jnp.arange(half, dtype=x.dtype) / half)
            sinusoid = pos[:, None] * inv_freq[None, :]
            sin, cos = (jnp.sin(sinusoid), jnp.cos(sinusoid))
            x1, x2 = (x[..., :half], x[..., half:])
            return jnp.concatenate([x1 * cos - x2 * sin, x2 * cos + x1 * sin], axis=-1)
        key = jax.random.key(seed)
        ks = jax.random.split(key, 8)
        B, N, D, QK, H = (4, 1024, 256, 64, 512)
        s = 0.02
        return {'x': jax.random.normal(ks[0], (B, N, D), dtype=jnp.float32), 'ln1_w': jnp.ones((D,), jnp.float32), 'ln1_b': jnp.zeros((D,), jnp.float32), 'Wqk': jax.random.normal(ks[1], (QK, D), jnp.float32) * s, 'bqk': jnp.zeros((QK,), jnp.float32), 'Wv': jax.random.normal(ks[2], (H, D), jnp.float32) * s, 'bv': jnp.zeros((H,), jnp.float32), 'Wg': jax.random.normal(ks[3], (H, D), jnp.float32) * s, 'bg': jnp.zeros((H,), jnp.float32), 'Wo': jax.random.normal(ks[4], (D, H), jnp.float32) * s, 'bo': jnp.zeros((D,), jnp.float32), 'ln2_w': jnp.ones((D,), jnp.float32), 'ln2_b': jnp.zeros((D,), jnp.float32), 'gamma': jax.random.normal(ks[5], (4, QK), jnp.float32) * 0.02, 'beta': jnp.zeros((4, QK), jnp.float32), 'pos_emb': jax.random.normal(ks[6], (2 * MAX_REL + 1,), jnp.float32)}
    _L0_attn_all = _L0_attn_setup()
    _L0_attn_in = {k: v for k, v in _L0_attn_all.items() if k in ('ln1_w', 'ln1_b', 'Wqk', 'bqk', 'Wv', 'bv', 'Wg', 'bg', 'Wo', 'bo', 'ln2_w', 'ln2_b', 'gamma', 'beta', 'pos_emb')}
    del _L0_attn_all

    def _L0_ffn_setup():
        import jax, jax.numpy as jnp
        import numpy as np
        CAPACITY_FACTOR = 0.5
        key = jax.random.key(seed)
        ks = jax.random.split(key, 5)
        B, S, D, F = (4, 1024, 256, 1024)
        scale_in = 1.0 / np.sqrt(D)
        scale_ff = 1.0 / np.sqrt(F)
        return {'hidden_states': jax.random.normal(ks[0], (B, S, D), dtype=jnp.float32), 'w_router': jax.random.normal(ks[1], (D,), dtype=jnp.float32) * scale_in, 'W1': jax.random.normal(ks[2], (D, F), dtype=jnp.float32) * scale_in, 'b1': jnp.zeros((F,), dtype=jnp.float32), 'W2': jax.random.normal(ks[3], (F, D), dtype=jnp.float32) * scale_ff, 'b2': jnp.zeros((D,), dtype=jnp.float32)}
    _L0_ffn_all = _L0_ffn_setup()
    _L0_ffn_in = {k: v for k, v in _L0_ffn_all.items() if k in ('w_router', 'W1', 'b1', 'W2', 'b2')}
    del _L0_ffn_all
    return {'x': x, 'L0_tok_emb_0': _L0_tok_in['emb_0'], 'L0_tok_proj_0': _L0_tok_in['proj_0'], 'L0_tok_emb_1': _L0_tok_in['emb_1'], 'L0_tok_proj_1': _L0_tok_in['proj_1'], 'L0_tok_emb_2': _L0_tok_in['emb_2'], 'L0_tok_proj_2': _L0_tok_in['proj_2'], 'L0_tok_emb_3': _L0_tok_in['emb_3'], 'L0_tok_proj_3': _L0_tok_in['proj_3'], 'L0_attn_ln1_w': _L0_attn_in['ln1_w'], 'L0_attn_ln1_b': _L0_attn_in['ln1_b'], 'L0_attn_Wqk': _L0_attn_in['Wqk'], 'L0_attn_bqk': _L0_attn_in['bqk'], 'L0_attn_Wv': _L0_attn_in['Wv'], 'L0_attn_bv': _L0_attn_in['bv'], 'L0_attn_Wg': _L0_attn_in['Wg'], 'L0_attn_bg': _L0_attn_in['bg'], 'L0_attn_Wo': _L0_attn_in['Wo'], 'L0_attn_bo': _L0_attn_in['bo'], 'L0_attn_ln2_w': _L0_attn_in['ln2_w'], 'L0_attn_ln2_b': _L0_attn_in['ln2_b'], 'L0_attn_gamma': _L0_attn_in['gamma'], 'L0_attn_beta': _L0_attn_in['beta'], 'L0_attn_pos_emb': _L0_attn_in['pos_emb'], 'L0_ffn_w_router': _L0_ffn_in['w_router'], 'L0_ffn_W1': _L0_ffn_in['W1'], 'L0_ffn_b1': _L0_ffn_in['b1'], 'L0_ffn_W2': _L0_ffn_in['W2'], 'L0_ffn_b2': _L0_ffn_in['b2']}

def reference(x, L0_tok_emb_0, L0_tok_proj_0, L0_tok_emb_1, L0_tok_proj_1, L0_tok_emb_2, L0_tok_proj_2, L0_tok_emb_3, L0_tok_proj_3, L0_attn_ln1_w, L0_attn_ln1_b, L0_attn_Wqk, L0_attn_bqk, L0_attn_Wv, L0_attn_bv, L0_attn_Wg, L0_attn_bg, L0_attn_Wo, L0_attn_bo, L0_attn_ln2_w, L0_attn_ln2_b, L0_attn_gamma, L0_attn_beta, L0_attn_pos_emb, L0_ffn_w_router, L0_ffn_W1, L0_ffn_b1, L0_ffn_W2, L0_ffn_b2):
    import jax
    import jax.numpy as jnp

    def _L0_tok_ref(inp, emb_0, proj_0, emb_1, proj_1, emb_2, proj_2, emb_3, proj_3):
        import jax, jax.numpy as jnp
        import numpy as np
        VOCAB = 32000
        D_EMBED = 256
        D_PROJ = 256
        DIV_VAL = 4
        CUTOFFS = [5000, 10000, 25000, VOCAB]
        CUT_ENDS = [0] + CUTOFFS
        embs = [emb_0, emb_1, emb_2, emb_3]
        projs = [proj_0, proj_1, proj_2, proj_3]
        flat = inp.reshape(-1)
        out = jnp.zeros((flat.shape[0], D_PROJ), jnp.float32)
        for i in range(len(CUTOFFS)):
            l, r = (CUT_ENDS[i], CUT_ENDS[i + 1])
            mask = (flat >= l) & (flat < r)
            idx = jnp.clip(flat - l, 0, r - l - 1)
            e = jnp.einsum('nd,pd->np', embs[i][idx], projs[i])
            out = out + jnp.where(mask[:, None], e, jnp.zeros((), e.dtype))
        emb_scale = jnp.asarray(D_PROJ ** 0.5, out.dtype)
        return (out * emb_scale).reshape(inp.shape + (D_PROJ,))

    def _L0_attn_ref(x, ln1_w, ln1_b, Wqk, bqk, Wv, bv, Wg, bg, Wo, bo, ln2_w, ln2_b, gamma, beta, pos_emb):
        import jax, jax.numpy as jnp
        import numpy as np
        GROUP = 64
        MAX_REL = 32

        def _silu(x):
            return x * jax.nn.sigmoid(x)

        def _ln(x, w, b, eps=1e-05):
            m = x.mean(-1, keepdims=True)
            v = ((x - m) ** 2).mean(-1, keepdims=True)
            return (x - m) / jnp.sqrt(v + eps) * w + b

        def _rope(x):
            n, d = (x.shape[-2], x.shape[-1])
            half = d // 2
            pos = jnp.arange(n, dtype=x.dtype)
            inv_freq = 10000.0 ** (-jnp.arange(half, dtype=x.dtype) / half)
            sinusoid = pos[:, None] * inv_freq[None, :]
            sin, cos = (jnp.sin(sinusoid), jnp.cos(sinusoid))
            x1, x2 = (x[..., :half], x[..., half:])
            return jnp.concatenate([x1 * cos - x2 * sin, x2 * cos + x1 * sin], axis=-1)
        b, n, d = x.shape
        G = GROUP
        x = _ln(x, ln1_w, ln1_b)
        qk = _silu(x @ Wqk.T + bqk)
        v = _silu(x @ Wv.T + bv)
        heads = qk[..., None, :] * gamma + beta
        quad_q, lin_q, quad_k, lin_k = (heads[..., i, :] for i in range(4))
        quad_q, lin_q, quad_k, lin_k = map(_rope, (quad_q, lin_q, quad_k, lin_k))
        g = n // G
        rs = lambda t: t.reshape(b, g, G, t.shape[-1])
        qq, lq, qkk, lk, vg = map(rs, (quad_q, lin_q, quad_k, lin_k, v))
        idx = jnp.arange(G)
        dist = jnp.clip(jnp.abs(idx[:, None] - idx[None, :]), 0, MAX_REL)
        bias = pos_emb[dist]
        quad_att = jnp.einsum('bgid,bgjd->bgij', qq, qkk) / G + bias
        attn = jax.nn.relu(quad_att) ** 2
        quad_out = jnp.einsum('bgij,bgje->bgie', attn, vg)
        lin_kv = jnp.einsum('bgnd,bgne->bde', lk, vg) / n
        lin_out = jnp.einsum('bgnd,bde->bgne', lq, lin_kv)
        qo = quad_out.reshape(b, n, -1)
        lo = lin_out.reshape(b, n, -1)
        gate = _silu(x @ Wg.T + bg)
        out = gate * (qo + lo)
        out = out @ Wo.T + bo
        return _ln(out, ln2_w, ln2_b)

    def _L0_ffn_ref(hidden_states, w_router, W1, b1, W2, b2):
        import jax, jax.numpy as jnp
        import numpy as np
        CAPACITY_FACTOR = 0.5
        'Mixture-of-Depths block: route top-k tokens through an FFN inner block,\n            scatter back with sigmoid router weights; bypassed tokens pass through.'
        B, S, D = hidden_states.shape
        k = int(S * CAPACITY_FACTOR)
        scores = jnp.einsum('bsd,d->bs', hidden_states, w_router)
        top_scores, top_idx = jax.lax.top_k(scores, k)
        weights = jax.nn.sigmoid(top_scores)
        selected = jnp.take_along_axis(hidden_states, top_idx[:, :, None], axis=1)
        h = jax.nn.gelu(jnp.einsum('bkd,df->bkf', selected, W1) + b1)
        processed = jnp.einsum('bkf,fd->bkd', h, W2) + b2
        update = weights[:, :, None] * processed

        def scatter_one(xb, ib, ub):
            return xb.at[ib].add(ub)
        output = jax.vmap(scatter_one)(hidden_states, top_idx, update)
        return output
    h = _L0_tok_ref(x, L0_tok_emb_0, L0_tok_proj_0, L0_tok_emb_1, L0_tok_proj_1, L0_tok_emb_2, L0_tok_proj_2, L0_tok_emb_3, L0_tok_proj_3)
    h = h + _L0_attn_ref(_layernorm(h, axis=-1), L0_attn_ln1_w, L0_attn_ln1_b, L0_attn_Wqk, L0_attn_bqk, L0_attn_Wv, L0_attn_bv, L0_attn_Wg, L0_attn_bg, L0_attn_Wo, L0_attn_bo, L0_attn_ln2_w, L0_attn_ln2_b, L0_attn_gamma, L0_attn_beta, L0_attn_pos_emb)
    h = h + _L0_ffn_ref(_layernorm(h, axis=-1), L0_ffn_w_router, L0_ffn_W1, L0_ffn_b1, L0_ffn_W2, L0_ffn_b2)
    return h

_drawn_inputs = setup_inputs


def setup_inputs(seed=0):
    import zlib

    import numpy as np

    out = dict(_drawn_inputs(seed))
    spreads = {'L0_attn_ln1_w': (1.0, 0.2),
     'L0_attn_ln1_b': (0.0, 0.1),
     'L0_attn_bqk': (0.0, 2.0),
     'L0_attn_bv': (0.0, 0.1),
     'L0_attn_bg': (0.0, 0.1),
     'L0_attn_bo': (0.0, 0.1),
     'L0_attn_ln2_w': (1.0, 0.2),
     'L0_attn_ln2_b': (0.0, 0.1),
     'L0_attn_beta': (0.0, 0.8),
     'L0_ffn_b1': (0.0, 0.8),
     'L0_ffn_b2': (0.0, 0.8)}
    factors = {'L0_attn_Wqk': 25.475, 'L0_attn_gamma': 8.0}
    for name, (base, spread) in spreads.items():
        noise = np.random.default_rng([zlib.crc32(name.encode()), seed]).standard_normal(out[name].shape)
        drawn = base * np.exp(spread * noise) if base else spread * noise
        out[name] = jnp.asarray(drawn.astype(out[name].dtype))
    for name, factor in factors.items():
        out[name] = (out[name] * factor).astype(out[name].dtype)
    return out
```

```python
from contextlib import ExitStack

import numpy as np
import concourse.bass as bass
from concourse import mybir

ALU = mybir.AluOpType
ACT = mybir.ActivationFunctionType
AX = mybir.AxisListType
F32 = mybir.dt.float32
F32R = mybir.dt.float32r
I32 = mybir.dt.int32

P = 128
BATCHES, SEQ = 16, 512
TILES = SEQ // P
VOCAB = 32000
WIDTHS = (256, 64, 16, 4)
ROW = sum(WIDTHS)
EC = 3
D, DC = 256, 2
QK, GROUP, MAX_REL = 64, 64, 32
H, HC = 512, 4
F, FC = 1024, 8
TOP = 256
EPS = 1e-5
RING = 3


def build(nc, a, out):
    ctx = ExitStack()
    with ctx:
        def sb(name, shape, dt=F32):
            return ctx.enter_context(nc.sbuf_tensor(name, shape, dt))

        def sem(name):
            return ctx.enter_context(nc.semaphore(name))

        def pair(name, shape):
            return (sb(name + "_hi", shape, F32R), sb(name + "_lo", shape, F32R))

        w_proj = pair("w_proj", [P, EC, D])
        w_qk = pair("w_qk", [P, DC, 2, P])
        w_v = pair("w_v", [P, DC, H])
        w_g = pair("w_g", [P, DC, H])
        w_o = pair("w_o", [P, HC, D])
        w_1 = pair("w_1", [P, DC, F])
        w_2 = pair("w_2", [P, FC, D])
        ident = sb("ident", [P, P])
        before = sb("before", [P, P])
        slots = sb("slots", [P, TOP])
        slot_of = sb("slot_of", [P, 2])
        cos = sb("cos", [P, SEQ])
        sin = sb("sin", [P, SEQ])
        head_gain = sb("head_gain", [P, 4])
        head_bias = sb("head_bias", [P, 4])
        rel_bias = sb("rel_bias", [P, GROUP])
        rel_row = sb("rel_row", [1, 2 * GROUP])
        pos_row = sb("pos_row", [1, MAX_REL + 1])
        ln1_w = sb("ln1_w", [P, DC])
        ln1_b = sb("ln1_b", [P, DC])
        b_qk = sb("b_qk", [P, 2])
        b_g = sb("b_g", [P, HC])
        b_1 = sb("b_1", [P, FC])
        bv_rows = sb("bv_rows", [P, H], F32R)
        ones = sb("ones", [P, P], F32R)
        bo_all = sb("bo_all", [P, D])
        ln2w_all = sb("ln2w_all", [P, D])
        ln2b_all = sb("ln2b_all", [P, D])
        b2_all = sb("b2_all", [P, D])
        router_all = sb("router_all", [P, D])
        neg_half = sb("neg_half", [P, TILES])
        ids = sb("ids", [P, (BATCHES + 1) * TILES], I32)
        ids_now = sb("ids_now", [P, TILES], I32)
        rows = sb("rows", [P, TILES, EC * P])
        rowsT = pair("rowsT", [P, 2, EC * P])
        h = sb("h", [P, TILES, D])
        h_plus = sb("h_plus", [P, TILES, D])
        z = sb("z", [P, 2, D])
        zT = pair("zT", [P, DC, SEQ])
        stats = [sb(f"stats{i}", [P, TILES, 6]) for i in range(3)]
        mv = [sb(f"mv{i}", [P, TILES, 2]) for i in range(3)]
        arg = [sb(f"arg{i}", [P, TILES]) for i in range(3)]
        rstd = [sb(f"rstd{i}", [P, TILES]) for i in range(3)]
        qk_or_prod = sb("qk_or_prod", [P, 2, SEQ])
        rope_or_x2 = sb("rope_or_x2", [P, 2, SEQ])
        x2 = rope_or_x2[:, :, :].rearrange("p a (b d) -> p (a b) d", d=D)
        heads = sb("heads", [P, 2, SEQ])
        lq = pair("lq", [GROUP, SEQ])
        lk = pair("lk", [P, TILES, QK])
        v = sb("v", [P, TILES, H])
        vy = pair("v_or_y", [P, 1024])
        v_split = [x[:, :].rearrange("p (a n) -> p a n", a=2) for x in vy]
        y_split = [x[:, :].rearrange("p (a n) -> p a n", a=TILES) for x in vy]
        attnT = sb("attnT", [P, TILES, P])
        kv = pair("kv", [QK, H])
        gate = sb("gate", [P, 2, SEQ])
        gated = pair("gated", [P, HC, SEQ])
        y = sb("y", [P, 2, D])
        base = sb("base", [P, TILES, D])
        junk = sb("junk", [P, SEQ])
        junk8 = junk[:, :].bitcast(mybir.dt.uint8)
        pre = junk[:, 0:TILES * GROUP].rearrange("p (t x) -> p t x", x=GROUP)
        score = sb("score", [P, TILES])
        counts = sb("counts", [P, TILES, 3])
        rank = sb("rank", [P, TILES])
        pick = sb("pick", [P, TILES, TOP], F32R)
        half_tanh = sb("half_tanh", [P, TILES])
        weight = sb("weight", [P, TILES])
        put = sb("put", [P, 2, SEQ], F32R)
        ys = pair("ys", [P, DC, TOP])
        act = sb("act", [P, 2, TOP])
        hid = pair("hid", [P, RING, TOP])
        upd = sb("upd", [P, 2, D])
        updp = pair("updp", [P, 2, D])
        ob = sb("ob", [P, 2, D])

        ps = ctx.enter_context(nc.psum_tensor("ps", [P, 8, 512], F32))
        rel_dram = nc.dram_tensor("rel_scratch", [2 * GROUP], F32, kind="Internal").ap()

        PER = {}

        def S(name, per):
            PER[name] = per
            return name

        sems = {}
        for name, per in dict(
            rowsT_ps=4, rows_hi=4, rows_lo=4, h_ps=2, h=2, h_plus=1,
            stat0=4, mv0=4, arg0=1, rstd0=1, stat1=4, mv1=4, arg1=1, rstd1=1,
            stat2=4, mv2=4, arg2=1, rstd2=1,
            z=4, zT_ps=4, zT_hi=2, zT_lo=2,
            qk_ps=2, qk=2, scaled=4, rope=6, lq_hi=1, lq_lo=1,
            v_ps=4, v=4, v_hi=4, v_lo=4, gate_ps=4, gate=4,
            lkT_ps=1, lk_hi=1, lk_lo=1, quad_ps=1, pre=2, attn=2,
            kv_ps=4, kv_hi=1, kv_lo=1, out_ps=4, prod=4, gated_hi=4, gated_lo=4,
            wo_ps=2, x2=2, t2=4, h2=4, y=4, y_hi=4, y_lo=4, score=4, base=4,
            srow_ps=1, count=11, rank=1, pick=4, tanh=1, weight=1,
            rrow_ps=1, put=2, ys_ps=1, ys_hi=1, ys_lo=1,
            ff1_ps=4, act=8, hid_hi=8, hid_lo=8, ff2_ps=8, upd=1, upd_hi=1, upd_lo=1,
            put_ps=2, res=4, ids=1,
        ).items():
            PER[name] = per
            sems[name] = sem("s_" + name)
        gathered = [sem(f"s_gathered{t}") for t in range(TILES)]
        stored = [sem(f"s_stored{i}") for i in range(2)]
        s_const = sem("s_const")
        s_pos = sem("s_pos")
        s_rel_row = sem("s_rel_row")
        s_rel_dram = sem("s_rel_dram")
        s_rel = sem("s_rel")
        s_cast = sem("s_cast")
        s_pool_set = sem("s_pool_set")
        s_set = sem("s_set")
        s_stage = {k: sem("s_stage_" + k) for k in ("proj", "qk", "v", "g", "o", "w1", "w2")}
        s_raw_used = sem("s_raw_used")
        s_scaled = sem("s_wscaled")
        s_bias = sem("s_bias")
        s_whi = sem("s_whi")
        s_wlo = sem("s_wlo")

        def after(eng, name, b, k=None):
            per = PER[name]
            k = per - 1 if k is None else k
            if isinstance(b, int) and b < 0:
                return
            eng.wait_ge(sems[name], b * per + (k + 1))

        def item(eng, name, b, k):
            per = PER[name]
            if k < 0:
                after(eng, name, b - 1, k + per)
            else:
                after(eng, name, b, k)

        def after_apart(eng, name, b, k=None):
            k = PER[name] - 1 if k is None else k
            value = b * PER[name] + (k + 1)
            if not isinstance(b, int):
                value = eng.snap(value)
            eng.wait_ge(s_const, N_CONST)
            eng.wait_ge(sems[name], value)

        def done(ins, name):
            ins.then_inc(sems[name], 1)

        def f32(ap):
            return ap.bitcast(F32)

        def mm3(eng, o, lhs, rhs, start, stop, shared=False):
            eng.matmul(o, lhs[0], rhs[0], start=start, stop=False, skip_group_check=shared)
            eng.matmul(o, lhs[1], rhs[0], start=False, stop=False, skip_group_check=shared)
            return eng.matmul(o, lhs[0], rhs[1], start=False, stop=stop, skip_group_check=shared)

        def both(p, f):
            return f(p[0]), f(p[1])

        def tok(t):
            return slice(P * t, P * t + P)

        def half(t):
            return slice(D * (t % 2), D * (t % 2) + D)

        raw_proj = gate[:, :, :].rearrange("p a n -> p (a n)")[:, 0:EC * D].rearrange("p (c n) -> p c n", c=EC)
        raw_qk = base[:, 0:2, :].rearrange("p a n -> p (a n)").rearrange("p (c j n) -> p c j n", c=DC, j=2)
        raw_v = qk_or_prod
        raw_g = rope_or_x2
        raw_o = h_plus
        raw_1 = v[:, :, :].rearrange("p a n -> p (a n)").rearrange("p (c n) -> p c n", c=DC)
        raw_2 = v[:, :, :].rearrange("p a n -> p (a n)").rearrange("p (c n) -> p c n", c=FC)
        bv_raw = junk[0:1, :]
        bv_sum = upd[0:1, :, :].rearrange("p a n -> p (a n)")
        N_SPLIT = 7

        consts = [
            (ids[:, 0:BATCHES * TILES], a["ids"]), (ident[:, :], a["ident"]), (before[:, :], a["before"]),
            (slots[:, :], a["slots"]), (slot_of[:, :], a["slot_of"]),
            (cos[:, :], a["cos"]), (sin[:, :], a["sin"]),
            (head_gain[:, :], a["head_gain"]), (head_bias[:, :], a["head_bias"]),
            (ln1_w[:, :], a["ln1_w"]), (ln1_b[:, :], a["ln1_b"]),
            (b_qk[:, :], a["b_qk"]), (b_g[:, :], a["b_g"]), (b_1[:, :], a["b_1"]),
            (bv_raw, a["b_v"]),
            (bo_all[:, :], a["b_o"].partition_broadcast(P)), (ln2w_all[:, :], a["ln2_w"].partition_broadcast(P)),
            (ln2b_all[:, :], a["ln2_b"].partition_broadcast(P)), (b2_all[:, :], a["b_2"].partition_broadcast(P)),
            (router_all[:, :], a["router"].partition_broadcast(P)),
        ]
        N_CONST = 16 * len(consts)

        block = ctx.enter_context(nc.Block())

        @block.sync
        def _(sp):
            sp.dma_start(pos_row[:, :], a["pos"]).then_inc(s_pos, 16)
            for dst, src in consts:
                sp.dma_start(dst, src).then_inc(s_const, 16)
            for k, dst in (("proj", raw_proj), ("qk", raw_qk), ("v", raw_v[:, :, :]), ("g", raw_g[:, :, :]),
                           ("w1", raw_1), ("o", raw_o[:, :, :])):
                sp.dma_start(dst, a["w_" + k]).then_inc(s_stage[k], 16)
            sp.wait_ge(s_rel_row, 3)
            sp.dma_start(rel_dram, rel_row[0, :]).then_inc(s_rel_dram, 16)
            sp.wait_ge(s_rel_dram, 16)
            for g in range(2):
                for i in range(GROUP):
                    sp.dma_start(rel_bias[GROUP * g + i:GROUP * g + i + 1, :],
                                 rel_dram[GROUP - 1 - i:2 * GROUP - 1 - i].unsqueeze(0)).then_inc(s_rel, 16)
            sp.wait_ge(s_whi, 5)
            sp.wait_ge(s_wlo, 5)
            sp.dma_start(raw_2, a["w_w2"]).then_inc(s_stage["w2"], 16)

            def store(b):
                for t in range(TILES):
                    after(sp, "res", b, t)
                    sp.dma_start(out[bass.ds(b * SEQ + P * t, P), :], ob[:, t % 2, :]).then_inc(stored[t % 2], 16)

            with sp.Fori(0, BATCHES) as b:
                store(b)
            for i in range(2):
                sp.wait_ge(stored[i], 16 * 2 * BATCHES)

        @block.gpsimd
        def _(pool):
            pool.memset(neg_half[:, :], -0.5).then_inc(s_pool_set, 1)
            pool.memset(rows[:, :, :], 0.0).then_inc(s_pool_set, 1)
            pool.memset(attnT[:, :, :], 0.0).then_inc(s_pool_set, 1)
            pool.wait_ge(s_cast, 1)
            pool.wait_ge(s_pool_set, 3)

            def gather(b):
                if not (isinstance(b, int) and b == 0):
                    for t in range(TILES):
                        pool.wait_ge(gathered[t], 16 * b)
                    after(pool, "rowsT_ps", b - 1)
                done(pool.tensor_copy(ids_now[:, :], ids[:, bass.ds(b * TILES, TILES)]), "ids")
                after(pool, "ids", b)
                add_ln2b(b - 1)
                for t in range(TILES):
                    pool.indirect_dma_start(
                        rows[:, t, 0:ROW], None, a["table"],
                        bass.IndirectOffsetOnAxis(ap=ids_now[:, t:t + 1].bitcast(mybir.dt.uint32), axis=0),
                    ).then_inc(gathered[t], 16)

            def root(i, b):
                after(pool, f"arg{i}", b)
                after(pool, ("z", "h2", "y")[i], b - 1)
                done(pool.tensor_tensor(rstd[i][:, :], arg[i][:, :], neg_half[:, :], ALU.pow), f"rstd{i}")

            def add_ln2b(b):
                if isinstance(b, int) and b < 0:
                    return
                after(pool, "h", b)
                after(pool, "h2", b - 1)
                done(pool.tensor_tensor(h_plus[:, :, :], h[:, :, :],
                                        ln2b_all[:, :].unsqueeze(1).to_broadcast([P, TILES, D]), ALU.add), "h_plus")

            def add_base(b):
                for t in range(TILES):
                    after(pool, "y", b, t)
                    after(pool, "res", b - 1)
                    done(pool.tensor_tensor(base[:, t, :], x2[:, t, :], y[:, t % 2, :], ALU.add), "base")

            pool.wait_ge(s_const, N_CONST)
            gather(0)
            root(0, 0)
            pool.wait_ge(s_whi, N_SPLIT)
            pool.wait_ge(s_wlo, N_SPLIT)
            gather(1)

            def step(b, last=False):
                root(1, b)
                if not last:
                    root(0, b + 1)
                root(2, b)
                add_base(b)
                if not last:
                    gather(b + 2)

            step(0)
            step(1)
            with pool.Fori(2, BATCHES - 1) as b:
                step(b)
            step(BATCHES - 1, last=True)

        @block.scalar
        def _(sc):
            sc.wait_ge(s_stage["proj"], 16)
            sc.activation(w_proj[0][:, :, :], raw_proj, ACT.Copy).then_inc(s_whi, 1)
            for i, (w, raw) in enumerate(((w_qk, raw_qk), (w_v, raw_v[:, :, :]), (w_g, raw_g[:, :, :]))):
                sc.wait_ge(s_scaled, DC * (i + 1))
                sc.activation(w[0][(slice(None),) * (4 if i == 0 else 3)], raw, ACT.Copy).then_inc(s_whi, 1)
            for k, w, raw in (("w1", w_1, raw_1), ("o", w_o, raw_o[:, :, :]), ("w2", w_2, raw_2)):
                sc.wait_ge(s_stage[k], 16)
                sc.activation(w[0][:, :, :], raw, ACT.Copy).then_inc(s_whi, 1)

            def rows_hi(b, t):
                after(sc, "rowsT_ps", b, t)
                if t < 2:
                    after(sc, "h_ps", b - 1)
                else:
                    after(sc, "h_ps", b, 0)
                done(sc.activation(rowsT[0][:, t % 2, :], ps[:, t % 2, 0:EC * P], ACT.Copy), "rows_hi")

            def take_h(b, p):
                after(sc, "h_ps", b, p)
                after(sc, "z", b - 1)
                after(sc, "h_plus", b - 1)
                done(sc.activation(h[:, 2 * p:2 * p + 2, :], ps[:, 2 + p, :].rearrange("p (t n) -> p t n", t=2),
                                   ACT.Copy, scale=float(D ** 0.5)), "h")

            def embed1(b):
                rows_hi(b, 0)
                rows_hi(b, 1)
                rows_hi(b, 2)
                rows_hi(b, 3)
                take_h(b, 0)
                take_h(b, 1)

            def embed2(b):
                for p in range(2):
                    after(sc, "zT_ps", b, 2 * p + 1)
                    after(sc, "gate_ps", b - 1)
                    done(sc.activation(
                        zT[0][:, :, D * p:D * p + D].rearrange("p c (t x) -> p t c x", x=P),
                        ps[:, p, :].rearrange("p (t c x) -> p t c x", t=2, c=DC), ACT.Copy), "zT_hi")

            def take_qk(b):
                for j in range(2):
                    after(sc, "qk_ps", b, j)
                    after(sc, "gated_lo", b - 1)
                    done(sc.activation(qk_or_prod[:, j, :], ps[:, j, :], ACT.Silu, bias=b_qk[:, j:j + 1]), "qk")
                for p in range(2):
                    for j in range(2):
                        if p == 0:
                            after(sc, "qk", b, j)
                            after(sc, "y", b - 1)
                            after(sc, "base", b - 1)
                        else:
                            after(sc, "rope", b, 2 if j else 0)
                        done(sc.activation(rope_or_x2[:, j, :], qk_or_prod[:, j, :], ACT.Identity,
                                           bias=head_bias[:, 2 * p + j:2 * p + j + 1],
                                           scale=head_gain[:, 2 * p + j:2 * p + j + 1]), "scaled")

            def take_v(b):
                for t in range(TILES):
                    after(sc, "v_ps", b, t)
                    after(sc, "out_ps", b - 1)
                    done(sc.activation(v[:, t, :], ps[:, 2 + t % 2, :], ACT.Silu), "v")

            def take_gate(b, e):
                after(sc, "gate_ps", b, e)
                item(sc, "prod", b, e - 2)
                done(sc.activation(gate[:, e % 2, :], ps[:, e % 2, :], ACT.Silu, bias=b_g[:, e:e + 1]), "gate")

            def take_ys(b):
                after(sc, "ys_ps", b)
                after(sc, "ff1_ps", b - 1)
                done(sc.activation(ys[0][:, :, :], ps[:, 6, :].rearrange("p (c n) -> p c n", c=DC), ACT.Copy), "ys_hi")

            def gelu(b):
                for f in range(FC):
                    after(sc, "ff1_ps", b, f // 2)
                    item(sc, "hid_lo", b, f - 2)
                    done(sc.activation(act[:, f % 2, :], ps[:, 5 + 2 * (f // 2 % 2), half(f)], ACT.Gelu_apprx_tanh,
                                       bias=b_1[:, f:f + 1]), "act")

            def take_lk(b):
                after(sc, "lkT_ps", b)
                after(sc, "kv_ps", b - 1)
                done(sc.activation(lk[0][:, :, :], ps[:, 4, 0:TILES * QK].rearrange("p (t c) -> p t c", c=QK),
                                   ACT.Copy), "lk_hi")

            def take_kv(b):
                after(sc, "kv_ps", b)
                after(sc, "out_ps", b - 1)
                done(sc.activation(kv[0][:, :], ps[0:QK, 3, :], ACT.Copy), "kv_hi")

            def router_tanh(b):
                after(sc, "score", b)
                after(sc, "weight", b - 1)
                done(sc.activation(half_tanh[:, :], score[:, :], ACT.Tanh, scale=0.5), "tanh")

            sc.wait_ge(s_const, N_CONST)
            embed1(0)
            embed2(0)
            sc.wait_ge(s_bias, 3)
            sc.wait_ge(s_wlo, N_SPLIT)

            def step(b, first=False, last=False):
                take_qk(b)
                take_v(b)
                if not first:
                    take_ys(b - 1)
                take_gate(b, 0)
                take_gate(b, 1)
                if not first:
                    gelu(b - 1)
                take_lk(b)
                take_kv(b)
                take_gate(b, 2)
                take_gate(b, 3)
                if not last:
                    embed1(b + 1)
                    embed2(b + 1)
                router_tanh(b)

            step(0, first=True)
            step(1)
            with sc.Fori(2, BATCHES - 1) as b:
                step(b)
            step(BATCHES - 1, last=True)
            take_ys(BATCHES - 1)
            gelu(BATCHES - 1)

        @block.vector
        def _(ve):
            ve.wait_ge(s_const, N_CONST)
            ve.memset(ids[:, BATCHES * TILES:], VOCAB).then_inc(s_set, 1)
            ve.tensor_scalar(ids[:, 0:BATCHES * TILES], ids[:, 0:BATCHES * TILES].bitcast(mybir.dt.uint32),
                             float(VOCAB), None, ALU.min).then_inc(s_cast, 1)
            ve.wait_ge(s_pos, 16)
            mid = GROUP - 1
            far = pos_row[0:1, MAX_REL:MAX_REL + 1]
            ve.tensor_copy(rel_row[0:1, mid:mid + MAX_REL + 1], pos_row[0:1, :]).then_inc(s_rel_row, 1)
            for k in range(1, MAX_REL + 1):
                ve.tensor_copy(rel_row[0:1, mid - k:mid - k + 1], pos_row[0:1, k:k + 1])
            ve.tensor_copy(rel_row[0:1, 0:mid - MAX_REL], far.to_broadcast([1, mid - MAX_REL])).then_inc(s_rel_row, 1)
            ve.tensor_copy(rel_row[0:1, mid + MAX_REL + 1:], far.to_broadcast([1, 2 * GROUP - mid - MAX_REL - 1])
                           ).then_inc(s_rel_row, 1)
            ve.memset(f32(bv_rows[:, :]), 0.0).then_inc(s_set, 1)
            ve.memset(f32(ones[:, :]), 1.0).then_inc(s_set, 1)
            ve.memset(counts[:, :, :], 0.0).then_inc(s_set, 1)
            ve.tensor_scalar(head_gain[0:QK, 2:4], head_gain[0:QK, 2:4], 1.0 / SEQ, None, ALU.mult).then_inc(s_set, 1)
            ve.tensor_scalar(head_bias[0:QK, 2:4], head_bias[0:QK, 2:4], 1.0 / SEQ, None, ALU.mult).then_inc(s_set, 1)
            ve.wait_ge(s_raw_used, 3)
            ve.tensor_tensor(b_qk[:, :], b_qk[:, :], ps[:, 3, 0:2], ALU.add).then_inc(s_bias, 1)
            ve.tensor_tensor(b_g[:, :], b_g[:, :], ps[:, 4, 0:HC], ALU.add).then_inc(s_bias, 1)
            ve.tensor_tensor(bv_sum, bv_raw, ps[0:1, 5, :], ALU.add).then_inc(s_bias, 1)
            ve.wait_ge(s_bias, 3)
            ve.wait_ge(s_set, 6)
            ve.tensor_copy(bv_rows[0:1, :], bv_sum).then_inc(s_bias, 1)
            ve.wait_ge(s_bias, 4)
            ve.tensor_tensor(bv_rows[32:33, :], bv_sum, f32(bv_rows[0:1, :]), ALU.subtract).then_inc(s_bias, 1)

            def split_lo(i, w, raw, nd=3):
                ix = (slice(None),) * nd
                ve.wait_ge(s_whi, i + 1)
                ve.tensor_tensor(w[1][ix], raw, f32(w[0][ix]), ALU.subtract).then_inc(s_wlo, 1)

            for raw, nd in ((raw_qk, 4), (raw_v, 3), (raw_g, 3)):
                for c in range(DC):
                    r = raw[:, c, :, :] if nd == 4 else raw[:, c, :]
                    ve.tensor_scalar(r, r, ln1_w[:, c:c + 1], None, ALU.mult).then_inc(s_scaled, 1)
            split_lo(0, w_proj, raw_proj)
            split_lo(1, w_qk, raw_qk, 4)
            split_lo(2, w_v, raw_v[:, :, :])
            split_lo(3, w_g, raw_g[:, :, :])
            split_lo(4, w_1, raw_1)
            split_lo(5, w_o, raw_o[:, :, :])

            def normal_stats(i, b, t, x):
                done(ve.bn_stats(stats[i][:, t, :], x), f"stat{i}")
                after_apart(ve, f"stat{i}", b, t)
                done(ve.bn_aggr(mv[i][:, t, :], stats[i][:, t, :]), f"mv{i}")

            def root_arg(i, b, scale, add):
                after(ve, f"mv{i}", b)
                after(ve, f"rstd{i}", b - 1)
                done(ve.tensor_scalar(arg[i][:, :], mv[i][:, :, 1], scale, add, ALU.mult, ALU.add), f"arg{i}")

            def rows_lo(b, t):
                after(ve, "rows_hi", b, t)
                done(ve.tensor_tensor(rowsT[1][:, t % 2, :], ps[:, t % 2, 0:EC * P], f32(rowsT[0][:, t % 2, :]),
                                      ALU.subtract), "rows_lo")

            def embed1(b):
                rows_lo(b, 0)
                rows_lo(b, 1)
                rows_lo(b, 2)
                rows_lo(b, 3)
                for t in range(TILES):
                    after(ve, "h", b, t // 2)
                    normal_stats(0, b, t, h[:, t, :])
                root_arg(0, b, 1.0 + EPS, EPS * EPS)

            def embed2(b):
                after(ve, "rstd0", b)
                for t in range(TILES):
                    item(ve, "zT_ps", b, t - 2)
                    done(ve.tensor_scalar(z[:, t % 2, :], h[:, t, :], mv[0][:, t, 0:1], rstd[0][:, t:t + 1],
                                          ALU.subtract, ALU.mult), "z")

            def embed3(b):
                for p in range(2):
                    after(ve, "zT_hi", b, p)
                    o = zT[1][:, :, D * p:D * p + D].rearrange("p c (t x) -> p t c x", x=P)
                    hi = f32(zT[0][:, :, D * p:D * p + D]).rearrange("p c (t x) -> p t c x", x=P)
                    done(ve.tensor_tensor(o, ps[:, p, :].rearrange("p (t c x) -> p t c x", t=2, c=DC), hi,
                                          ALU.subtract), "zT_lo")

            def rope(b):
                for p in range(2):
                    after(ve, "scaled", b, 2 * p)
                    after(ve, "quad_ps", b - 1)
                    after(ve, "lkT_ps", b - 1)
                    done(ve.tensor_tensor(heads[:, p, :], rope_or_x2[:, 0, :], cos[:, :], ALU.mult), "rope")
                    after(ve, "scaled", b, 2 * p + 1)
                    done(ve.tensor_tensor(rope_or_x2[:, 1, :], rope_or_x2[:, 1, :], sin[:, :], ALU.mult), "rope")
                    after(ve, "rope", b, 3 * p + 1)
                    done(ve.tensor_tensor(heads[:, p, :], heads[:, p, :], rope_or_x2[:, 1, :], ALU.add), "rope")
                    if p == 0:
                        after(ve, "rope", b, 2)
                        after(ve, "out_ps", b - 1)
                        done(ve.tensor_copy(lq[0][:, :], heads[0:QK, 0, :]), "lq_hi")
                        after(ve, "lq_hi", b)
                        done(ve.tensor_tensor(lq[1][:, :], heads[0:QK, 0, :], f32(lq[0][:, :]), ALU.subtract), "lq_lo")

            def take_rank_row(b):
                after(ve, "rrow_ps", b)
                after(ve, "put_ps", b - 1)
                for k in range(2):
                    done(ve.tensor_scalar(put[:, k, :], ps[:, 4, :], slot_of[:, k:k + 1], None, ALU.is_equal), "put")

            def take_ys(b):
                after(ve, "ys_ps", b)
                after(ve, "ff1_ps", b - 1)
                done(ve.tensor_copy(ys[1][:, :, :], ps[:, 7, :].rearrange("p (c n) -> p c n", c=DC)), "ys_lo")

            def split_hidden(b):
                for f in range(FC):
                    after(ve, "act", b, f)
                    item(ve, "ff2_ps", b, f - RING)
                    done(ve.tensor_copy(hid[0][:, f % RING, :], act[:, f % 2, :]), "hid_hi")
                    after(ve, "hid_hi", b, f)
                    done(ve.tensor_tensor(hid[1][:, f % RING, :], act[:, f % 2, :], f32(hid[0][:, f % RING, :]),
                                          ALU.subtract), "hid_lo")

            def split_update(b):
                after(ve, "ff2_ps", b)
                done(ve.tensor_tensor(upd[:, :, :], ps[:, 6, :].rearrange("p (k n) -> p k n", k=2),
                                      b2_all[:, :].unsqueeze(1).to_broadcast([P, 2, D]), ALU.add), "upd")
                after(ve, "upd", b)
                after(ve, "put_ps", b - 1)
                done(ve.tensor_copy(updp[0][:, :, :], upd[:, :, :]), "upd_hi")
                after(ve, "upd_hi", b)
                done(ve.tensor_tensor(updp[1][:, :, :], upd[:, :, :], f32(updp[0][:, :, :]), ALU.subtract), "upd_lo")

            def result(b):
                for t in range(TILES):
                    after(ve, "put_ps", b, t // 2)
                    after(ve, "base", b, t)
                    if t >= 2 or not (isinstance(b, int) and b == 0):
                        ve.wait_ge(stored[t % 2], (b * 2 + t // 2) * 16)
                    done(ve.scalar_tensor_tensor(ob[:, t % 2, :], ps[:, 5 + 2 * (t // 2), half(t)], weight[:, t:t + 1],
                                                 base[:, t, :], ALU.mult, ALU.add), "res")

            def quad(b):
                after(ve, "lk_hi", b)
                done(ve.tensor_tensor(lk[1][:, :, :], ps[:, 4, 0:TILES * QK].rearrange("p (t c) -> p t c", c=QK),
                                      f32(lk[0][:, :, :]), ALU.subtract), "lk_lo")
                after(ve, "quad_ps", b)
                blocks = [slice(GROUP * g, GROUP * g + GROUP) for g in range(2)]
                for g, r in enumerate(blocks):
                    done(ve.scalar_tensor_tensor(
                        pre[r, :, :], ps[r, 2, :].rearrange("p (t x) -> p t x", x=P)[:, :, r], 1.0 / GROUP,
                        rel_bias[r, :].unsqueeze(1).to_broadcast([GROUP, TILES, GROUP]), ALU.mult, ALU.add), "pre")
                after(ve, "out_ps", b - 1)
                for g, r in enumerate(blocks):
                    after(ve, "pre", b, g)
                    done(ve.scalar_tensor_tensor(attnT[r, :, r], pre[r, :, :], 0.0, pre[r, :, :],
                                                 ALU.max, ALU.mult), "attn")

            def split_v(b):
                after(ve, "ys_ps", b - 1)
                for t in range(TILES):
                    after(ve, "v", b, t)
                    item(ve, "kv_ps", b, t - 2)
                    done(ve.tensor_copy(v_split[0][:, t % 2, :], v[:, t, :]), "v_hi")
                    after(ve, "v_hi", b, t)
                    done(ve.tensor_tensor(v_split[1][:, t % 2, :], v[:, t, :], f32(v_split[0][:, t % 2, :]),
                                          ALU.subtract), "v_lo")
                after(ve, "kv_hi", b)
                done(ve.tensor_tensor(kv[1][:, :], ps[0:QK, 3, :], f32(kv[0][:, :]), ALU.subtract), "kv_lo")

            def take_out(b):
                for e in range(HC):
                    after(ve, "out_ps", b, e)
                    after(ve, "gate", b, e)
                    item(ve, "gated_lo", b, e - 2)
                    after(ve, "wo_ps", b - 1)
                    done(ve.tensor_tensor(qk_or_prod[:, e % 2, :], ps[:, 4 if e % 2 == 0 else 2, :],
                                          gate[:, e % 2, :], ALU.mult), "prod")
                    after(ve, "prod", b, e)
                    done(ve.tensor_copy(gated[0][:, e, :], qk_or_prod[:, e % 2, :]), "gated_hi")
                    after(ve, "gated_hi", b, e)
                    done(ve.tensor_tensor(gated[1][:, e, :], qk_or_prod[:, e % 2, :], f32(gated[0][:, e, :]),
                                          ALU.subtract), "gated_lo")

            def tail1(b):
                for p in range(2):
                    after(ve, "wo_ps", b, p)
                    done(ve.tensor_tensor(x2[:, 2 * p:2 * p + 2, :], ps[:, 3 + p, :].rearrange("p (t n) -> p t n", t=2),
                                          bo_all[:, :].unsqueeze(1).to_broadcast([P, 2, D]), ALU.add), "x2")
                    after(ve, "x2", b, p)
                    for t in range(2 * p, 2 * p + 2):
                        normal_stats(1, b, t, x2[:, t, :])
                root_arg(1, b, 1.0, EPS)

            def tail2(b):
                after(ve, "rstd1", b)
                after(ve, "h_plus", b)
                for t in range(TILES):
                    done(ve.scalar_tensor_tensor(x2[:, t, :], x2[:, t, :], mv[1][:, t, 0:1], ln2w_all[:, :],
                                                 ALU.subtract, ALU.mult), "t2")
                    after(ve, "t2", b, t)
                    done(ve.scalar_tensor_tensor(x2[:, t, :], x2[:, t, :], rstd[1][:, t:t + 1], h_plus[:, t, :],
                                                 ALU.mult, ALU.add), "h2")
                    after(ve, "h2", b, t)
                    normal_stats(2, b, t, x2[:, t, :])
                root_arg(2, b, 1.0, EPS)

            def tail3(b):
                after(ve, "rstd2", b)
                after(ve, "tanh", b - 1)
                after(ve, "kv_ps", b)
                for t in range(TILES):
                    item(ve, "base", b, t - 2)
                    done(ve.tensor_scalar(y[:, t % 2, :], x2[:, t, :], mv[2][:, t, 0:1], rstd[2][:, t:t + 1],
                                          ALU.subtract, ALU.mult), "y")
                    after(ve, "y", b, t)
                    done(ve.tensor_copy(y_split[0][:, t, :], y[:, t % 2, :]), "y_hi")
                    item(ve, "score", b, t - 2)
                    done(ve.tensor_tensor_reduce(junk[:, half(t)], y[:, t % 2, :], router_all[:, :], 1.0, 0.0,
                                                 ALU.mult, ALU.add, score[:, t:t + 1]), "score")
                    after(ve, "y_hi", b, t)
                    done(ve.tensor_tensor(y_split[1][:, t, :], y[:, t % 2, :], f32(y_split[0][:, t, :]),
                                          ALU.subtract), "y_lo")

            def ranks(b):
                after(ve, "srow_ps", b)
                for t in range(TILES):
                    s = score[:, t:t + 1]
                    if t >= 2:
                        after(ve, "count", b, (1, 4)[t - 2])
                    done(ve.tensor_scalar(junk8[:, SEQ * (t % 2) + P * t:SEQ * (t % 2) + SEQ], ps[:, 4, P * t:SEQ], s, 0.0, ALU.is_gt, ALU.add,
                                          accum_out=counts[:, t, 0:1]), "count")
                    if t:
                        done(ve.tensor_scalar(junk8[:, SEQ * (t % 2):SEQ * (t % 2) + P * t], ps[:, 4, 0:P * t], s, 0.0, ALU.is_ge, ALU.add,
                                              accum_out=counts[:, t, 1:2]), "count")
                    done(ve.scalar_tensor_tensor(junk8[:, 2 * SEQ + P * t:2 * SEQ + P * t + P], ps[:, 4, tok(t)], s, before[:, :], ALU.is_equal,
                                                 ALU.mult, accum_out=counts[:, t, 2:3]), "count")
                after(ve, "count", b)
                after(ve, "rrow_ps", b - 1)
                done(ve.tensor_reduce(rank[:, :], counts[:, :, :], AX.X, ALU.add), "rank")
                after(ve, "rank", b)
                after(ve, "ys_ps", b - 1)
                for t in range(TILES):
                    done(ve.tensor_scalar(pick[:, t, :], slots[:, :], rank[:, t:t + 1], None, ALU.is_equal), "pick")
                after(ve, "tanh", b)
                done(ve.tensor_scalar(weight[:, :], half_tanh[:, :], 0.5, 0.5, ALU.mult, ALU.add), "weight")

            embed1(0)
            embed2(0)
            embed3(0)
            split_lo(6, w_2, raw_2)
            ve.wait_ge(s_pool_set, 3)
            ve.wait_ge(s_rel, 16 * 2 * GROUP)

            def step(b, first=False, last=False):
                rope(b)
                if not first:
                    take_rank_row(b - 1)
                    take_ys(b - 1)
                    split_hidden(b - 1)
                    split_update(b - 1)
                quad(b)
                split_v(b)
                take_out(b)
                if not first:
                    result(b - 1)
                tail1(b)
                if not last:
                    embed1(b + 1)
                tail2(b)
                if not last:
                    embed2(b + 1)
                tail3(b)
                if not last:
                    embed3(b + 1)
                ranks(b)

            step(0, first=True)
            step(1)
            with ve.Fori(2, BATCHES - 1) as b:
                step(b)
            step(BATCHES - 1, last=True)
            take_rank_row(BATCHES - 1)
            take_ys(BATCHES - 1)
            split_hidden(BATCHES - 1)
            split_update(BATCHES - 1)
            result(BATCHES - 1)

        @block.tensor
        def _(pe):
            pe.wait_ge(s_const, N_CONST)
            pe.wait_ge(s_stage["qk"], 16)
            pe.wait_ge(s_stage["v"], 16)
            pe.wait_ge(s_stage["g"], 16)
            for j in range(2):
                for c in range(DC):
                    m = pe.matmul(ps[:, 3, j:j + 1], raw_qk[:, c, j, :], ln1_b[:, c:c + 1], start=(c == 0), stop=(c == 1))
            m.then_inc(s_raw_used, 1)
            for e in range(HC):
                for c in range(DC):
                    m = pe.matmul(ps[:, 4, e:e + 1], raw_g[:, c, tok(e)], ln1_b[:, c:c + 1], start=(c == 0), stop=(c == 1))
            m.then_inc(s_raw_used, 1)
            for c in range(DC):
                m = pe.matmul(ps[0:1, 5, :], ln1_b[:, c:c + 1], raw_v[:, c, :], start=(c == 0), stop=(c == 1))
            m.then_inc(s_raw_used, 1)

            def rows_T(b, t):
                pe.wait_ge(gathered[t], (b + 1) * 16)
                if t == 0:
                    after(pe, "gate", b - 1)
                if t >= 2:
                    after(pe, "rows_lo", b, t - 2)
                for c in range(EC):
                    m = pe.transpose(ps[:, t % 2, tok(c)], rows[:, t, tok(c)], ident[:, :])
                done(m, "rowsT_ps")

            def embed_mm(b, t):
                after(pe, "rows_lo", b, t)
                if t == 0:
                    after(pe, "prod", b - 1)
                if t == 2:
                    after(pe, "x2", b - 1, 0)
                for c in range(EC):
                    m = mm3(pe, ps[:, 2 + t // 2, half(t)], both(rowsT, lambda x: x[:, t % 2, tok(c)]),
                            both(w_proj, lambda x: x[:, c, :]), c == 0, c == EC - 1)
                if t % 2:
                    done(m, "h_ps")

            def embed1(b):
                rows_T(b, 0)
                rows_T(b, 1)
                embed_mm(b, 0)
                rows_T(b, 2)
                embed_mm(b, 1)
                rows_T(b, 3)
                embed_mm(b, 2)
                embed_mm(b, 3)

            def embed2(b):
                after(pe, "rows_lo", b)
                for t in range(TILES):
                    after(pe, "z", b, t)
                    for c in range(DC):
                        m = pe.transpose(ps[:, t // 2, D * (t % 2) + P * c:D * (t % 2) + P * c + P],
                                         z[:, t % 2, tok(c)], ident[:, :])
                    done(m, "zT_ps")

            def qk(b):
                after(pe, "zT_lo", b)
                for j in range(2):
                    for c in range(DC):
                        m = mm3(pe, ps[:, j, :], both(w_qk, lambda x: x[:, c, j, :]),
                                both(zT, lambda x: x[:, c, :]), c == 0, c == 1)
                    done(m, "qk_ps")

            def vs(b):
                after(pe, "h", b)
                for t in range(TILES):
                    if t >= 2:
                        after(pe, "v", b, t - 2)
                    pe.matmul(ps[:, 2 + t % 2, :], ones[:, :], bv_rows[:, :], start=True, stop=False)
                    for c in range(DC):
                        m = mm3(pe, ps[:, 2 + t % 2, :], both(zT, lambda x: x[:, c, tok(t)]),
                                both(w_v, lambda x: x[:, c, :]), False, c == 1)
                    done(m, "v_ps")

            def gates(b, e):
                if e < 2:
                    after(pe, "qk", b, e)
                else:
                    after(pe, "gate", b, e - 2)
                for c in range(DC):
                    m = mm3(pe, ps[:, e % 2, :], both(w_g, lambda x: x[:, c, tok(e)]),
                            both(zT, lambda x: x[:, c, :]), c == 0, c == 1)
                done(m, "gate_ps")

            def rank_row(b):
                after(pe, "rank", b)
                for t in range(TILES):
                    m = pe.transpose(ps[:, 4, tok(t)], rank[:, t:t + 1].to_broadcast([P, P]), ident[:, :])
                done(m, "rrow_ps")

            def select(b):
                after(pe, "pick", b)
                after(pe, "y_lo", b)
                after(pe, "upd", b - 1)
                for c in range(DC):
                    for part in range(2):
                        for t in range(TILES):
                            m = pe.matmul(ps[:, 6 + part, TOP * c:TOP * c + TOP], y_split[part][:, t, tok(c)],
                                          pick[:, t, :], start=(t == 0), stop=(t == TILES - 1))
                done(m, "ys_ps")

            def ff1(b, g):
                if g == 0:
                    after(pe, "ys_hi", b)
                    after(pe, "ys_lo", b)
                    after(pe, "res", b - 1)
                if g >= 2:
                    after(pe, "act", b, 2 * g - 3)
                for f in (2 * g, 2 * g + 1):
                    for c in range(DC):
                        m = mm3(pe, ps[:, 5 + 2 * (g % 2), half(f)], both(w_1, lambda x: x[:, c, tok(f)]),
                                both(ys, lambda x: x[:, c, :]), c == 0, c == 1)
                done(m, "ff1_ps")

            def ff2(b, f):
                after(pe, "hid_lo", b, f)
                for k in range(2):
                    for i, j in ((0, 0), (1, 0), (0, 1)):
                        m = pe.matmul(ps[:, 6, half(k)], hid[i][:, f % RING, tok(k)], w_2[j][:, f, :],
                                      start=(f == 0 and k == 0 and i + j == 0), stop=(f == FC - 1 and j == 1),
                                      skip_group_check=True)
                done(m, "ff2_ps")

            def ffn(b):
                ff1(b, 0)
                ff1(b, 1)
                for g in range(2, FC // 2):
                    ff2(b, 2 * g - 4)
                    ff2(b, 2 * g - 3)
                    ff1(b, g)
                for f in range(FC - 4, FC):
                    ff2(b, f)

            def put_back(b):
                after(pe, "upd_lo", b)
                after(pe, "put", b)
                after(pe, "act", b)
                for t in range(TILES):
                    n = 0
                    for k in range(2):
                        for part in range(2):
                            m = pe.matmul(ps[:, 5 + 2 * (t // 2), half(t)], put[:, k, tok(t)], updp[part][:, k, :],
                                          start=(n == 0), stop=(n == 3))
                            n += 1
                    if t % 2:
                        done(m, "put_ps")

            def quad(b):
                after(pe, "put", b - 1)
                after(pe, "rope", b)
                after(pe, "v", b, 2)
                for t in range(TILES):
                    m = pe.matmul(ps[:, 2, tok(t)], heads[QK:P, 1, tok(t)], heads[QK:P, 0, tok(t)],
                                  start=True, stop=True)
                done(m, "quad_ps")
                for t in range(TILES):
                    m = pe.transpose(ps[:, 4, QK * t:QK * t + QK], heads[0:QK, 1, tok(t)], ident[0:QK, 0:QK])
                done(m, "lkT_ps")

            def kvs(b):
                after(pe, "v", b, 3)
                after(pe, "lk_lo", b)
                for t in range(TILES):
                    after(pe, "v_lo", b, t)
                    m = mm3(pe, ps[0:QK, 3, :], both(lk, lambda x: x[:, t, :]),
                            [x[:, t % 2, :] for x in v_split], t == 0, t == TILES - 1)
                    done(m, "kv_ps")

            def outs(b, e):
                bank = 4 if e % 2 == 0 else 2
                if e == 0:
                    after(pe, "kv_lo", b)
                    after(pe, "lq_lo", b)
                    after(pe, "attn", b)
                if e >= 2:
                    after(pe, "prod", b, e - 2)
                mm3(pe, ps[:, bank, :], both(kv, lambda x: x[:, tok(e)]), both(lq, lambda x: x[:, :]), True, False, shared=True)
                for t in range(TILES):
                    m = pe.matmul(ps[:, bank, tok(t)], v[:, t, tok(e)], attnT[:, t, :],
                                  start=False, stop=True, skip_group_check=True)
                done(m, "out_ps")

            def project(b):
                after(pe, "gated_lo", b)
                for t in range(TILES):
                    for e in range(HC):
                        m = mm3(pe, ps[:, 3 + t // 2, half(t)], both(gated, lambda x: x[:, e, tok(t)]),
                                both(w_o, lambda x: x[:, e, :]), e == 0, e == HC - 1)
                    if t % 2:
                        done(m, "wo_ps")

            def score_row(b):
                after(pe, "score", b)
                after(pe, "x2", b)
                for t in range(TILES):
                    m = pe.transpose(ps[:, 4, tok(t)], score[:, t:t + 1].to_broadcast([P, P]), ident[:, :])
                done(m, "srow_ps")

            pe.wait_ge(s_wlo, 1)
            pe.wait_ge(s_set, 6)
            pe.wait_ge(s_pool_set, 3)
            pe.wait_ge(s_bias, 5)
            embed1(0)
            embed2(0)
            pe.wait_ge(s_wlo, N_SPLIT)

            def step(b, first=False, last=False):
                qk(b)
                vs(b)
                if not first:
                    rank_row(b - 1)
                    select(b - 1)
                gates(b, 0)
                gates(b, 1)
                if not first:
                    ffn(b - 1)
                quad(b)
                kvs(b)
                outs(b, 0)
                outs(b, 1)
                gates(b, 2)
                gates(b, 3)
                outs(b, 2)
                outs(b, 3)
                if not first:
                    put_back(b - 1)
                project(b)
                if not last:
                    embed1(b + 1)
                    embed2(b + 1)
                score_row(b)

            step(0, first=True)
            step(1)
            with pe.Fori(2, BATCHES - 1) as b:
                step(b)
            step(BATCHES - 1, last=True)
            rank_row(BATCHES - 1)
            select(BATCHES - 1)
            ffn(BATCHES - 1)
            put_back(BATCHES - 1)


def constants():
    half = QK // 2
    inv = (np.float32(10000.0) ** (-np.arange(half, dtype=np.float32) / np.float32(half))).astype(np.float32)
    ang = (np.arange(SEQ, dtype=np.float32)[:, None] * inv[None, :]).astype(np.float32)
    sin, cos = np.sin(ang).T, np.cos(ang).T
    return {
        "cos": np.concatenate([cos] * 4).astype(np.float32),
        "sin": np.concatenate([-sin, sin] * 2).astype(np.float32),
        "ident": np.eye(P, dtype=np.float32),
        "before": (np.arange(P)[None, :] < np.arange(P)[:, None]).astype(np.float32),
        "slots": np.tile(np.arange(TOP, dtype=np.float32), (P, 1)),
        "slot_of": (np.arange(P)[:, None] + P * np.arange(2)[None, :]).astype(np.float32),
    }


def kernel(**inputs):
    import concourse.bacc as bacc
    from concourse.bass_utils import run_bass_kernel_spmd

    g = {k: np.asarray(x) for k, x in inputs.items()}
    table = np.zeros((VOCAB + 1, ROW), np.float32)
    proj = np.zeros((EC * P, D), np.float32)
    row = col = 0
    for i, w in enumerate(WIDTHS):
        emb = g[f"L0_tok_emb_{i}"]
        table[row:row + emb.shape[0], col:col + w] = emb
        proj[col:col + w] = g[f"L0_tok_proj_{i}"].T
        row, col = row + emb.shape[0], col + w

    def rows_of(w, chunks):
        return np.ascontiguousarray(w.reshape(chunks, P, -1).transpose(1, 0, 2))

    def column(x, n):
        return np.ascontiguousarray(x.reshape(n, P).T)

    def swap(x):
        return np.concatenate([x[QK // 2:], x[:QK // 2]])

    wqk = g["L0_attn_Wqk"]
    wqk2 = np.concatenate([wqk, wqk, swap(wqk), swap(wqk)])

    def by_head(x):
        q, lq, k, lk = x
        cols = []
        for lin, quad in ((lq, q), (lk, k)):
            cols += [np.concatenate([lin, quad]), np.concatenate([swap(lin), swap(quad)])]
        return np.ascontiguousarray(np.stack(cols, 1))

    bqk = g["L0_attn_bqk"]
    arrays = {
        "ids": np.ascontiguousarray(g["x"].reshape(-1, P).T),
        "table": table,
        "w_proj": rows_of(proj, EC),
        "w_qk": np.ascontiguousarray(wqk2.T.reshape(DC, P, 2, P).transpose(1, 0, 2, 3)),
        "w_v": rows_of(g["L0_attn_Wv"].T, DC),
        "w_g": rows_of(g["L0_attn_Wg"].T, DC),
        "w_o": rows_of(g["L0_attn_Wo"].T, HC),
        "w_w1": rows_of(g["L0_ffn_W1"], DC),
        "w_w2": rows_of(g["L0_ffn_W2"], FC),
        "ln1_w": column(g["L0_attn_ln1_w"], DC),
        "ln1_b": column(g["L0_attn_ln1_b"], DC),
        "b_qk": column(np.concatenate([bqk, bqk, swap(bqk), swap(bqk)]), 2),
        "b_v": g["L0_attn_bv"].reshape(1, H),
        "b_g": column(g["L0_attn_bg"], HC),
        "b_1": column(g["L0_ffn_b1"], FC),
        "b_o": g["L0_attn_bo"],
        "b_2": g["L0_ffn_b2"],
        "ln2_w": g["L0_attn_ln2_w"],
        "ln2_b": g["L0_attn_ln2_b"],
        "router": g["L0_ffn_w_router"],
        "head_gain": by_head(g["L0_attn_gamma"]),
        "head_bias": by_head(g["L0_attn_beta"]),
        "pos": g["L0_attn_pos_emb"][:MAX_REL + 1].reshape(1, -1),
        **constants(),
    }
    nc = bacc.Bacc("TRN2", target_bir_lowering=False, num_devices=1)
    aps = {k: nc.dram_tensor("in_" + k, x.shape, mybir.dt.from_np(x.dtype), kind="ExternalInput").ap()
           for k, x in arrays.items()}
    out = nc.dram_tensor("out_0", (BATCHES * SEQ, D), F32, kind="ExternalOutput").ap()
    build(nc, aps, out)
    r = run_bass_kernel_spmd(nc, [{"in_" + k: x for k, x in arrays.items()}], core_ids=[0])
    return r.results[0]["out_0"].reshape(BATCHES, SEQ, D)
```

```python
from contextlib import ExitStack

import numpy as np
import concourse.bass as bass
from concourse import mybir

ALU = mybir.AluOpType
ACT = mybir.ActivationFunctionType
AX = mybir.AxisListType
F32 = mybir.dt.float32
F32R = mybir.dt.float32r
I32 = mybir.dt.int32

P = 128
BATCHES, SEQ = 16, 512
TILES = SEQ // P
VOCAB = 32000
WIDTHS = (256, 64, 16, 4)
ROW = sum(WIDTHS)
EC = 3
D, DC = 256, 2
QK, GROUP, MAX_REL = 64, 64, 32
H, HC = 512, 4
F, FC = 1024, 8
TOP = 256
EPS = 1e-5
RING = 3


def build(nc, a, out):
    ctx = ExitStack()
    with ctx:
        def sb(name, shape, dt=F32):
            return ctx.enter_context(nc.sbuf_tensor(name, shape, dt))

        def sem(name):
            return ctx.enter_context(nc.semaphore(name))

        def pair(name, shape):
            return (sb(name + "_hi", shape, F32R), sb(name + "_lo", shape, F32R))

        w_proj = pair("w_proj", [P, EC, D])
        w_qk = pair("w_qk", [P, DC, 2, P])
        w_v = pair("w_v", [P, DC, H])
        w_g = pair("w_g", [P, DC, H])
        w_o = pair("w_o", [P, HC, D])
        w_1 = pair("w_1", [P, DC, F])
        w_2 = pair("w_2", [P, FC, D])
        ident = sb("ident", [P, P])
        before = sb("before", [P, P])
        slots = sb("slots", [P, TOP])
        slot_of = sb("slot_of", [P, 2])
        cos = sb("cos", [P, SEQ])
        sin = sb("sin", [P, SEQ])
        head_gain = sb("head_gain", [P, 4])
        head_bias = sb("head_bias", [P, 4])
        rel_bias = sb("rel_bias", [P, GROUP])
        rel_row = sb("rel_row", [1, 2 * GROUP])
        pos_row = sb("pos_row", [1, MAX_REL + 1])
        ln1_w = sb("ln1_w", [P, DC])
        ln1_b = sb("ln1_b", [P, DC])
        b_qk = sb("b_qk", [P, 2])
        b_g = sb("b_g", [P, HC])
        b_1 = sb("b_1", [P, FC])
        bv_rows = sb("bv_rows", [P, H], F32R)
        ones = sb("ones", [P, P], F32R)
        bo_all = sb("bo_all", [P, D])
        ln2w_all = sb("ln2w_all", [P, D])
        ln2b_all = sb("ln2b_all", [P, D])
        b2_all = sb("b2_all", [P, D])
        router_all = sb("router_all", [P, D])
        neg_half = sb("neg_half", [P, TILES])
        ids = sb("ids", [P, (BATCHES + 1) * TILES], I32)
        ids_now = sb("ids_now", [P, TILES], I32)
        rows = sb("rows", [P, TILES, EC * P])
        rowsT = pair("rowsT", [P, 2, EC * P])
        h = sb("h", [P, TILES, D])
        h_plus = sb("h_plus", [P, TILES, D])
        z = sb("z", [P, 2, D])
        zT = pair("zT", [P, DC, SEQ])
        stats = [sb(f"stats{i}", [P, TILES, 6]) for i in range(3)]
        mv = [sb(f"mv{i}", [P, TILES, 2]) for i in range(3)]
        arg = [sb(f"arg{i}", [P, TILES]) for i in range(3)]
        rstd = [sb(f"rstd{i}", [P, TILES]) for i in range(3)]
        gate = sb("gate", [P, HC, SEQ])
        qk_act = gate[:, 2:4, :]
        x2 = gate[:, 0:2, :].rearrange("p a (b d) -> p (a b) d", d=D)
        scaled = sb("scaled", [P, 2, SEQ])
        heads = sb("heads", [P, 2, SEQ])
        lq = pair("lq", [GROUP, SEQ])
        lk = pair("lk", [P, TILES, QK])
        v = sb("v", [P, TILES, H])
        y_split = pair("y_split", [P, TILES, D])
        attnT = sb("attnT", [P, TILES, P])
        kv = pair("kv", [QK, H])
        v_or_gated = pair("v_or_gated", [P, HC, SEQ])
        v_split = gated = v_or_gated
        y = sb("y", [P, TILES, D])
        base = sb("base", [P, TILES, D])
        junk = sb("junk", [P, SEQ])
        junk8 = junk[:, :].bitcast(mybir.dt.uint8)
        pre = junk[:, 0:TILES * GROUP].rearrange("p (t x) -> p t x", x=GROUP)
        score = sb("score", [P, TILES])
        counts = sb("counts", [P, TILES, 3])
        rank = sb("rank", [P, TILES])
        pick = sb("pick", [P, TILES, TOP], F32R)
        half_tanh = sb("half_tanh", [P, TILES])
        weight = sb("weight", [P, TILES])
        put = sb("put", [P, 2, SEQ], F32R)
        ys = pair("ys", [P, DC, TOP])
        act = sb("act", [P, 2, TOP])
        hid = pair("hid", [P, RING, TOP])
        upd = sb("upd", [P, 2, D])
        updp = ys
        ob = sb("ob", [P, TILES, D])

        ps = ctx.enter_context(nc.psum_tensor("ps", [P, 8, 512], F32))
        rel_dram = nc.dram_tensor("rel_scratch", [GROUP, 2 * GROUP], F32, kind="Internal").ap()

        PER = {}

        def S(name, per):
            PER[name] = per
            return name

        sems = {}
        for name, per in dict(
            rowsT_ps=4, rows_hi=4, rows_lo=4, h_ps=2, h=2, h_plus=1,
            stat0=4, mv0=4, arg0=1, rstd0=1, stat1=4, mv1=4, arg1=1, rstd1=1,
            stat2=4, mv2=4, arg2=1, rstd2=1,
            z=4, zT_ps=4, zT_hi=2, zT_lo=2,
            qk_ps=2, qk=2, scaled=4, rope=6, lq_hi=1, lq_lo=1,
            v_ps=4, v=4, v_hi=4, v_lo=4, gate_ps=4, gate=4,
            lkT_ps=1, lk_hi=1, lk_lo=1, quad_ps=1, pre=2, attn=2,
            kv_ps=4, kv_hi=1, kv_lo=1, out_ps=4, prod=4, gated_hi=4, gated_lo=4,
            wo_ps=2, x2=2, t2=4, h2=4, y=4, y_hi=2, y_lo=2, score=4, base=4,
            srow_ps=1, count=11, rank=1, pick=4, tanh=1, weight=1,
            rrow_ps=1, put=2, ys_ps=1, ys_hi=1, ys_lo=1,
            ff1_ps=4, act=8, hid_hi=8, hid_lo=8, ff2_ps=8, upd=1, upd_hi=1, upd_lo=1,
            put_ps=2, res=4, stored=1, ids=1,
        ).items():
            PER[name] = per
            sems[name] = sem("s_" + name)
        gathered = [sem(f"s_gathered{t}") for t in range(TILES)]
        s_const = sem("s_const")
        s_pos = sem("s_pos")
        s_rel_row = sem("s_rel_row")
        s_rel_dram = sem("s_rel_dram")
        s_rel = sem("s_rel")
        s_cast = sem("s_cast")
        s_pool_set = sem("s_pool_set")
        s_set = sem("s_set")
        s_stage = {k: sem("s_stage_" + k) for k in ("proj", "qk", "v", "g", "o", "w1", "w2")}
        s_raw_used = sem("s_raw_used")
        s_scaled = sem("s_wscaled")
        s_bias = sem("s_bias")
        s_whi = sem("s_whi")
        s_wlo = sem("s_wlo")

        def after(eng, name, b, k=None):
            per = PER[name]
            k = per - 1 if k is None else k
            if isinstance(b, int) and b < 0:
                return
            eng.wait_ge(sems[name], b * per + (k + 1))

        def item(eng, name, b, k):
            per = PER[name]
            if k < 0:
                after(eng, name, b - 1, k + per)
            else:
                after(eng, name, b, k)

        def after_apart(eng, name, b, k=None):
            k = PER[name] - 1 if k is None else k
            value = b * PER[name] + (k + 1)
            if not isinstance(b, int):
                value = eng.snap(value)
            eng.wait_ge(s_const, N_CONST)
            eng.wait_ge(sems[name], value)

        def done(ins, name):
            ins.then_inc(sems[name], 1)

        def f32(ap):
            return ap.bitcast(F32)

        def mm3(eng, o, lhs, rhs, start, stop, shared=False):
            eng.matmul(o, lhs[0], rhs[0], start=start, stop=False, skip_group_check=shared)
            eng.matmul(o, lhs[1], rhs[0], start=False, stop=False, skip_group_check=shared)
            return eng.matmul(o, lhs[0], rhs[1], start=False, stop=stop, skip_group_check=shared)

        def both(p, f):
            return f(p[0]), f(p[1])

        def tok(t):
            return slice(P * t, P * t + P)

        def half(t):
            return slice(D * (t % 2), D * (t % 2) + D)

        raw_proj = gate[:, 0:2, :].rearrange("p a n -> p (a n)")[:, 0:EC * D].rearrange("p (c n) -> p c n", c=EC)
        raw_qk = base[:, 0:2, :].rearrange("p a n -> p (a n)").rearrange("p (c j n) -> p c j n", c=DC, j=2)
        raw_v = gate[:, 2:4, :]
        raw_g = scaled[:, :, :]
        raw_o = ob[:, :, :]
        raw_1 = v[:, :, :].rearrange("p a n -> p (a n)").rearrange("p (c n) -> p c n", c=DC)
        raw_2 = [x[:, :, :].rearrange("p a n -> p (a n)").rearrange("p (c n) -> p c n", c=FC // 2)
                 for x in (heads, y)]
        bv_raw = junk[0:1, :]
        bv_sum = upd[0:1, :, :].rearrange("p a n -> p (a n)")
        N_SPLIT = 8

        consts = [
            (ids[:, 0:BATCHES * TILES], a["ids"]), (ident[:, :], a["ident"]), (before[:, :], a["before"]),
            (slots[:, :], a["slots"]), (slot_of[:, :], a["slot_of"]),
            (cos[:, :], a["cos"]), (sin[:, :], a["sin"]),
            (head_gain[:, :], a["head_gain"]), (head_bias[:, :], a["head_bias"]),
            (ln1_w[:, :], a["ln1_w"]), (ln1_b[:, :], a["ln1_b"]),
            (b_qk[:, :], a["b_qk"]), (b_g[:, :], a["b_g"]), (b_1[:, :], a["b_1"]),
            (bv_raw, a["b_v"]),
            (bo_all[:, :], a["b_o"].partition_broadcast(P)), (ln2w_all[:, :], a["ln2_w"].partition_broadcast(P)),
            (ln2b_all[:, :], a["ln2_b"].partition_broadcast(P)), (b2_all[:, :], a["b_2"].partition_broadcast(P)),
            (router_all[:, :], a["router"].partition_broadcast(P)),
        ]
        N_CONST = 16 * len(consts)

        block = ctx.enter_context(nc.Block())

        @block.sync
        def _(sp):
            sp.dma_start(pos_row[:, :], a["pos"]).then_inc(s_pos, 16)
            for dst, src in consts:
                sp.dma_start(dst, src).then_inc(s_const, 16)
            for k, dst in (("proj", raw_proj), ("qk", raw_qk), ("v", raw_v), ("g", raw_g),
                           ("w1", raw_1), ("o", raw_o)):
                sp.dma_start(dst, a["w_" + k]).then_inc(s_stage[k], 16)
            for i in range(2):
                sp.dma_start(raw_2[i], a["w_w2"][:, bass.ts(i, FC // 2), :]).then_inc(s_stage["w2"], 16)
            sp.wait_ge(s_rel_row, 3)
            sp.dma_start(rel_dram, rel_row[0:1, :].unsqueeze(1).to_broadcast([1, GROUP, 2 * GROUP])).then_inc(s_rel_dram, 16)
            sp.wait_ge(s_rel_dram, 16)
            for g in range(2):
                rows_back = bass.AP(rel_dram.tensor, GROUP - 1, [[2 * GROUP - 1, GROUP], [1, GROUP]])
                sp.dma_start(rel_bias[GROUP * g:GROUP * g + GROUP, :], rows_back).then_inc(s_rel, 16)

            with sp.Fori(0, BATCHES) as b:
                after(sp, "res", b)
                sp.dma_start(out[bass.ds(b * SEQ, SEQ), :].rearrange("(t p) d -> p t d", p=P), ob[:, :, :]
                             ).then_inc(sems["stored"], 16)
            sp.wait_ge(sems["stored"], 16 * BATCHES)

        @block.gpsimd
        def _(pool):
            pool.memset(neg_half[:, :], -0.5).then_inc(s_pool_set, 1)
            pool.memset(rows[:, :, :], 0.0).then_inc(s_pool_set, 1)
            pool.memset(attnT[:, :, :], 0.0).then_inc(s_pool_set, 1)
            pool.wait_ge(s_cast, 1)
            pool.wait_ge(s_pool_set, 3)

            def gather(b, between=None):
                if not (isinstance(b, int) and b == 0):
                    for t in range(TILES):
                        pool.wait_ge(gathered[t], 16 * b)
                    after(pool, "rowsT_ps", b - 1)
                done(pool.tensor_copy(ids_now[:, :], ids[:, bass.ds(b * TILES, TILES)]), "ids")
                after(pool, "ids", b)
                if between:
                    between()
                for t in range(TILES):
                    pool.indirect_dma_start(
                        rows[:, t, 0:ROW], None, a["table"],
                        bass.IndirectOffsetOnAxis(ap=ids_now[:, t:t + 1].bitcast(mybir.dt.uint32), axis=0),
                    ).then_inc(gathered[t], 16)

            def root(i, b):
                after(pool, f"arg{i}", b)
                after(pool, ("z", "h2", "y")[i], b - 1)
                done(pool.tensor_tensor(rstd[i][:, :], arg[i][:, :], neg_half[:, :], ALU.pow), f"rstd{i}")

            def add_ln2b(b):
                after(pool, "h", b)
                after(pool, "h2", b - 1)
                done(pool.tensor_tensor(h_plus[:, :, :], h[:, :, :],
                                        ln2b_all[:, :].unsqueeze(1).to_broadcast([P, TILES, D]), ALU.add), "h_plus")

            def add_base(b):
                after(pool, "res", b - 1)
                for t in range(TILES):
                    after(pool, "y", b, t)
                    done(pool.tensor_tensor(base[:, t, :], x2[:, t, :], y[:, t, :], ALU.add), "base")

            pool.wait_ge(s_const, N_CONST)
            gather(0)
            root(0, 0)
            gather(1)

            def step(b, first=False, last=False):
                if not first:
                    root(2, b - 1)
                add_ln2b(b)
                if not first:
                    add_base(b - 1)
                if not last:
                    gather(b + 2, lambda: root(0, b + 1))
                root(1, b)

            step(0, first=True)
            step(1)
            with pool.Fori(2, BATCHES - 1) as b:
                step(b)
            step(BATCHES - 1, last=True)
            root(2, BATCHES - 1)
            add_base(BATCHES - 1)

        @block.scalar
        def _(sc):
            sc.wait_ge(s_stage["proj"], 16)
            sc.activation(w_proj[0][:, :, :], raw_proj, ACT.Copy).then_inc(s_whi, 1)
            for i, (w, raw) in enumerate(((w_qk, raw_qk), (w_v, raw_v), (w_g, raw_g))):
                sc.wait_ge(s_scaled, DC * (i + 1))
                sc.activation(w[0][(slice(None),) * (4 if i == 0 else 3)], raw, ACT.Copy).then_inc(s_whi, 1)
            for k, w, raw in (("w1", w_1, raw_1), ("o", w_o, raw_o)):
                sc.wait_ge(s_stage[k], 16)
                sc.activation(w[0][:, :, :], raw, ACT.Copy).then_inc(s_whi, 1)
            sc.wait_ge(s_stage["w2"], 32)
            for i in range(2):
                sc.activation(w_2[0][:, bass.ts(i, FC // 2), :], raw_2[i], ACT.Copy).then_inc(s_whi, 1)

            def rows_hi(b, t):
                after(sc, "rowsT_ps", b, t)
                if t < 2:
                    after(sc, "h_ps", b - 1)
                else:
                    after(sc, "h_ps", b, 0)
                done(sc.activation(rowsT[0][:, t % 2, :], ps[:, 0, 0:EC * P], ACT.Copy), "rows_hi")

            def take_h(b, p):
                after(sc, "h_ps", b, p)
                after(sc, "z", b - 1)
                after(sc, "h_plus", b - 1)
                done(sc.activation(h[:, 2 * p:2 * p + 2, :], ps[:, 1, :].rearrange("p (t n) -> p t n", t=2),
                                   ACT.Copy, scale=float(D ** 0.5)), "h")

            def zT_hi(b, p):
                after(sc, "zT_ps", b, 2 * p + 1)
                after(sc, "gate_ps", b - 1)
                done(sc.activation(
                    zT[0][:, :, D * p:D * p + D].rearrange("p c (t x) -> p t c x", x=P),
                    ps[:, p, :].rearrange("p (t c x) -> p t c x", t=2, c=DC), ACT.Copy), "zT_hi")

            def take_qk(b, j):
                after(sc, "qk_ps", b, j)
                after(sc, "gated_lo", b - 1)
                done(sc.activation(qk_act[:, j, :], ps[:, j, :], ACT.Silu, bias=b_qk[:, j:j + 1]), "qk")

            def scale_heads(b, p):
                for j in range(2):
                    if p == 0:
                        after(sc, "qk", b, j)
                        after(sc, "rope", b - 1)
                    else:
                        after(sc, "rope", b, 2 if j else 0)
                    done(sc.activation(scaled[:, j, :], qk_act[:, j, :], ACT.Identity,
                                       bias=head_bias[:, 2 * p + j:2 * p + j + 1],
                                       scale=head_gain[:, 2 * p + j:2 * p + j + 1]), "scaled")

            def take_v(b, ts):
                for t in ts:
                    after(sc, "v_ps", b, t)
                    after(sc, "out_ps", b - 1)
                    done(sc.activation(v[:, t, :], ps[:, 2 + t % 2, :], ACT.Silu), "v")

            def take_gate(b, e):
                after(sc, "gate_ps", b, e)
                if e < 2:
                    after(sc, "base", b - 1)
                else:
                    after(sc, "scaled", b)
                done(sc.activation(gate[:, e, :], ps[:, e % 2, :], ACT.Silu, bias=b_g[:, e:e + 1]), "gate")

            def take_ys(b):
                after(sc, "ys_ps", b)
                done(sc.activation(ys[0][:, :, :], ps[:, 6, :].rearrange("p (c n) -> p c n", c=DC), ACT.Copy), "ys_hi")

            def y_hi(b, p):
                after(sc, "y", b, 2 * p + 1)
                after(sc, "ys_ps", b - 1)
                done(sc.activation(y_split[0][:, 2 * p:2 * p + 2, :], y[:, 2 * p:2 * p + 2, :], ACT.Copy), "y_hi")

            def upd_hi(b):
                after(sc, "upd", b)
                done(sc.activation(updp[0][:, :, :], upd[:, :, :], ACT.Copy), "upd_hi")

            def gelu(b, f):
                after(sc, "ff1_ps", b, f // 2)
                item(sc, "hid_lo", b, f - 2)
                item(sc, "hid_hi", b, f - 2)
                done(sc.activation(act[:, f % 2, :], ps[:, 5 + 2 * (f // 2 % 2), half(f)], ACT.Gelu_apprx_tanh,
                                   bias=b_1[:, f:f + 1]), "act")
                after(sc, "act", b, f)
                item(sc, "ff2_ps", b, f - RING)
                done(sc.activation(hid[0][:, f % RING, :], act[:, f % 2, :], ACT.Copy), "hid_hi")

            def take_lk(b):
                after(sc, "lkT_ps", b)
                after(sc, "kv_ps", b - 1)
                done(sc.activation(lk[0][:, :, :], ps[:, 4, 0:TILES * QK].rearrange("p (t c) -> p t c", c=QK),
                                   ACT.Copy), "lk_hi")

            def v_hi(b, ts):
                for t in ts:
                    after(sc, "v", b, t)
                    done(sc.activation(v_split[0][:, t, :], v[:, t, :], ACT.Copy), "v_hi")

            def gated_hi(b, e):
                after(sc, "prod", b, e)
                after(sc, "kv_ps", b)
                done(sc.activation(gated[0][:, e, :], gate[:, e, :], ACT.Copy), "gated_hi")

            def take_kv(b):
                after(sc, "kv_ps", b)
                after(sc, "out_ps", b - 1)
                done(sc.activation(kv[0][:, :], ps[0:QK, 3, :], ACT.Copy), "kv_hi")

            def router_tanh(b):
                after(sc, "score", b)
                after(sc, "weight", b - 1)
                done(sc.activation(half_tanh[:, :], score[:, :], ACT.Tanh, scale=0.5), "tanh")

            sc.wait_ge(s_const, N_CONST)
            rows_hi(0, 0)
            rows_hi(0, 1)
            take_h(0, 0)
            rows_hi(0, 2)
            rows_hi(0, 3)
            take_h(0, 1)
            zT_hi(0, 0)
            zT_hi(0, 1)
            sc.wait_ge(s_bias, 3)
            sc.wait_ge(s_wlo, N_SPLIT)

            def step(b, first=False, second=False, last=False):
                more = not last
                if not first and not second:
                    upd_hi(b - 2)
                if not first:
                    y_hi(b - 1, 0)
                take_qk(b, 0)
                if not first:
                    y_hi(b - 1, 1)
                take_qk(b, 1)
                scale_heads(b, 0)
                take_v(b, (0, 1))
                scale_heads(b, 1)
                take_v(b, (2, 3))
                take_gate(b, 0)
                take_gate(b, 1)
                v_hi(b, (0, 1))
                if not first:
                    take_ys(b - 1)
                v_hi(b, (2,))
                take_gate(b, 2)
                v_hi(b, (3,))
                take_lk(b)
                take_gate(b, 3)
                take_kv(b)
                if not first:
                    router_tanh(b - 1)
                    gelu(b - 1, 0)
                    gelu(b - 1, 1)
                if more:
                    rows_hi(b + 1, 0)
                gated_hi(b, 0)
                if not first:
                    gelu(b - 1, 2)
                if more:
                    rows_hi(b + 1, 1)
                gated_hi(b, 1)
                if not first:
                    gelu(b - 1, 3)
                if more:
                    rows_hi(b + 1, 2)
                    take_h(b + 1, 0)
                gated_hi(b, 2)
                if more:
                    rows_hi(b + 1, 3)
                gated_hi(b, 3)
                if not first:
                    gelu(b - 1, 4)
                    gelu(b - 1, 5)
                if more:
                    take_h(b + 1, 1)
                if not first:
                    gelu(b - 1, 6)
                if more:
                    zT_hi(b + 1, 0)
                if not first:
                    gelu(b - 1, 7)
                if more:
                    zT_hi(b + 1, 1)

            step(0, first=True)
            step(1, second=True)
            with sc.Fori(2, BATCHES - 1) as b:
                step(b)
            step(BATCHES - 1, last=True)
            upd_hi(BATCHES - 2)
            y_hi(BATCHES - 1, 0)
            y_hi(BATCHES - 1, 1)
            router_tanh(BATCHES - 1)
            take_ys(BATCHES - 1)
            for f in range(FC):
                gelu(BATCHES - 1, f)
            upd_hi(BATCHES - 1)

        @block.vector
        def _(ve):
            ve.wait_ge(s_const, N_CONST)
            ve.memset(ids[:, BATCHES * TILES:], VOCAB).then_inc(s_set, 1)
            ve.tensor_scalar(ids[:, 0:BATCHES * TILES], ids[:, 0:BATCHES * TILES].bitcast(mybir.dt.uint32),
                             float(VOCAB), None, ALU.min).then_inc(s_cast, 1)
            ve.wait_ge(s_pos, 16)
            mid = GROUP - 1
            far = pos_row[0:1, MAX_REL:MAX_REL + 1]
            ve.tensor_copy(rel_row[0:1, mid:mid + MAX_REL + 1], pos_row[0:1, :]).then_inc(s_rel_row, 1)
            for k in range(1, MAX_REL + 1):
                ve.tensor_copy(rel_row[0:1, mid - k:mid - k + 1], pos_row[0:1, k:k + 1])
            ve.tensor_copy(rel_row[0:1, 0:mid - MAX_REL], far.to_broadcast([1, mid - MAX_REL])).then_inc(s_rel_row, 1)
            ve.tensor_copy(rel_row[0:1, mid + MAX_REL + 1:], far.to_broadcast([1, 2 * GROUP - mid - MAX_REL - 1])
                           ).then_inc(s_rel_row, 1)
            ve.memset(f32(bv_rows[:, :]), 0.0).then_inc(s_set, 1)
            ve.memset(f32(ones[:, :]), 1.0).then_inc(s_set, 1)
            ve.memset(counts[:, :, :], 0.0).then_inc(s_set, 1)
            ve.tensor_scalar(head_gain[0:QK, 2:4], head_gain[0:QK, 2:4], 1.0 / SEQ, None, ALU.mult).then_inc(s_set, 1)
            ve.tensor_scalar(head_bias[0:QK, 2:4], head_bias[0:QK, 2:4], 1.0 / SEQ, None, ALU.mult).then_inc(s_set, 1)
            ve.wait_ge(s_raw_used, 3)
            ve.tensor_tensor(b_qk[:, :], b_qk[:, :], ps[:, 3, 0:2], ALU.add).then_inc(s_bias, 1)
            ve.tensor_tensor(b_g[:, :], b_g[:, :], ps[:, 4, 0:HC], ALU.add).then_inc(s_bias, 1)
            ve.tensor_tensor(bv_sum, bv_raw, ps[0:1, 5, :], ALU.add).then_inc(s_bias, 1)
            ve.wait_ge(s_bias, 3)
            ve.wait_ge(s_set, 6)
            ve.tensor_copy(bv_rows[0:1, :], bv_sum).then_inc(s_bias, 1)
            ve.wait_ge(s_bias, 4)
            ve.tensor_tensor(bv_rows[32:33, :], bv_sum, f32(bv_rows[0:1, :]), ALU.subtract).then_inc(s_bias, 1)

            def split_lo(i, w, raw, nd=3):
                ix = (slice(None),) * nd
                ve.wait_ge(s_whi, i + 1)
                ve.tensor_tensor(w[1][ix], raw, f32(w[0][ix]), ALU.subtract).then_inc(s_wlo, 1)

            for raw, nd in ((raw_qk, 4), (raw_v, 3), (raw_g, 3)):
                for c in range(DC):
                    r = raw[:, c, :, :] if nd == 4 else raw[:, c, :]
                    ve.tensor_scalar(r, r, ln1_w[:, c:c + 1], None, ALU.mult).then_inc(s_scaled, 1)
            split_lo(0, w_proj, raw_proj)
            split_lo(1, w_qk, raw_qk, 4)
            split_lo(2, w_v, raw_v)
            split_lo(3, w_g, raw_g)
            split_lo(4, w_1, raw_1)
            split_lo(5, w_o, raw_o)

            def normal_stats(i, b, p, x):
                for t in (2 * p, 2 * p + 1):
                    done(ve.bn_stats(stats[i][:, t, :], x(t)), f"stat{i}")
                after_apart(ve, f"stat{i}", b, 2 * p + 1)
                for t in (2 * p, 2 * p + 1):
                    done(ve.bn_aggr(mv[i][:, t, :], stats[i][:, t, :]), f"mv{i}")

            def root_arg(i, b, scale, add):
                after(ve, f"mv{i}", b)
                after(ve, f"rstd{i}", b - 1)
                done(ve.tensor_scalar(arg[i][:, :], mv[i][:, :, 1], scale, add, ALU.mult, ALU.add), f"arg{i}")

            def rows_lo(b, t):
                after(ve, "rows_hi", b, t)
                done(ve.tensor_tensor(rowsT[1][:, t % 2, :], ps[:, 0, 0:EC * P], f32(rowsT[0][:, t % 2, :]),
                                      ALU.subtract), "rows_lo")

            def h_stats(b, p):
                after(ve, "h", b, p)
                normal_stats(0, b, p, lambda t: h[:, t, :])
                if p == 1:
                    root_arg(0, b, 1.0 + EPS, EPS * EPS)

            def make_z(b, p):
                after(ve, "rstd0", b)
                for t in (2 * p, 2 * p + 1):
                    item(ve, "zT_ps", b, t - 2)
                    done(ve.tensor_scalar(z[:, t % 2, :], h[:, t, :], mv[0][:, t, 0:1], rstd[0][:, t:t + 1],
                                          ALU.subtract, ALU.mult), "z")

            def zT_lo(b, p):
                after(ve, "zT_hi", b, p)
                o = zT[1][:, :, D * p:D * p + D].rearrange("p c (t x) -> p t c x", x=P)
                hi = f32(zT[0][:, :, D * p:D * p + D]).rearrange("p c (t x) -> p t c x", x=P)
                done(ve.tensor_tensor(o, ps[:, p, :].rearrange("p (t c x) -> p t c x", t=2, c=DC), hi,
                                      ALU.subtract), "zT_lo")

            def rope(b, p):
                after(ve, "scaled", b, 2 * p)
                after(ve, "quad_ps", b - 1)
                after(ve, "lkT_ps", b - 1)
                done(ve.tensor_tensor(heads[:, p, :], scaled[:, 0, :], cos[:, :], ALU.mult), "rope")
                after(ve, "scaled", b, 2 * p + 1)
                done(ve.tensor_tensor(scaled[:, 1, :], scaled[:, 1, :], sin[:, :], ALU.mult), "rope")
                after(ve, "rope", b, 3 * p + 1)
                done(ve.tensor_tensor(heads[:, p, :], heads[:, p, :], scaled[:, 1, :], ALU.add), "rope")

            def split_lq(b):
                after(ve, "rope", b, 2)
                after(ve, "out_ps", b - 1)
                done(ve.tensor_copy(lq[0][:, :], heads[0:QK, 0, :]), "lq_hi")
                after(ve, "lq_hi", b)
                done(ve.tensor_tensor(lq[1][:, :], heads[0:QK, 0, :], f32(lq[0][:, :]), ALU.subtract), "lq_lo")

            def take_rank_row(b):
                after(ve, "rrow_ps", b)
                after(ve, "put_ps", b - 1)
                for k in range(2):
                    done(ve.tensor_scalar(put[:, k, :], ps[:, 4, :], slot_of[:, k:k + 1], None, ALU.is_equal), "put")

            def take_ys(b):
                after(ve, "ys_ps", b)
                done(ve.tensor_copy(ys[1][:, :, :], ps[:, 7, :].rearrange("p (c n) -> p c n", c=DC)), "ys_lo")

            def split_hidden(b, fs):
                for f in fs:
                    after(ve, "hid_hi", b, f)
                    done(ve.tensor_tensor(hid[1][:, f % RING, :], act[:, f % 2, :], f32(hid[0][:, f % RING, :]),
                                          ALU.subtract), "hid_lo")

            def split_update(b):
                after(ve, "ff2_ps", b)
                done(ve.tensor_tensor(upd[:, :, :], ps[:, 6, :].rearrange("p (k n) -> p k n", k=2),
                                      b2_all[:, :].unsqueeze(1).to_broadcast([P, 2, D]), ALU.add), "upd")
                after(ve, "upd_hi", b)
                done(ve.tensor_tensor(updp[1][:, :, :], upd[:, :, :], f32(updp[0][:, :, :]), ALU.subtract), "upd_lo")

            def result(b):
                for t in range(TILES):
                    after(ve, "put_ps", b, t // 2)
                    after(ve, "base", b, t)
                    if t == 0 and not (isinstance(b, int) and b == 0):
                        ve.wait_ge(sems["stored"], b * 16)
                    done(ve.scalar_tensor_tensor(ob[:, t, :], ps[:, 5 + 2 * (t // 2), half(t)], weight[:, t:t + 1],
                                                 base[:, t, :], ALU.mult, ALU.add), "res")

            def take_lk(b):
                after(ve, "lk_hi", b)
                done(ve.tensor_tensor(lk[1][:, :, :], ps[:, 4, 0:TILES * QK].rearrange("p (t c) -> p t c", c=QK),
                                      f32(lk[0][:, :, :]), ALU.subtract), "lk_lo")

            def take_quad(b):
                after(ve, "quad_ps", b)
                blocks = [slice(GROUP * g, GROUP * g + GROUP) for g in range(2)]
                for g, r in enumerate(blocks):
                    done(ve.scalar_tensor_tensor(
                        pre[r, :, :], ps[r, 2, :].rearrange("p (t x) -> p t x", x=P)[:, :, r], 1.0 / GROUP,
                        rel_bias[r, :].unsqueeze(1).to_broadcast([GROUP, TILES, GROUP]), ALU.mult, ALU.add), "pre")
                after(ve, "out_ps", b - 1)
                for g, r in enumerate(blocks):
                    after(ve, "pre", b, g)
                    done(ve.scalar_tensor_tensor(attnT[r, :, r], pre[r, :, :], 0.0, pre[r, :, :],
                                                 ALU.max, ALU.mult), "attn")

            def split_v(b, ts):
                for t in ts:
                    after(ve, "v_hi", b, t)
                    done(ve.tensor_tensor(v_split[1][:, t, :], v[:, t, :], f32(v_split[0][:, t, :]),
                                          ALU.subtract), "v_lo")

            def split_kv(b):
                after(ve, "kv_hi", b)
                done(ve.tensor_tensor(kv[1][:, :], ps[0:QK, 3, :], f32(kv[0][:, :]), ALU.subtract), "kv_lo")

            def take_out(b, e):
                after(ve, "out_ps", b, e)
                after(ve, "gate", b, e)
                done(ve.tensor_tensor(gate[:, e, :], ps[:, 4 if e % 2 == 0 else 2, :], gate[:, e, :], ALU.mult), "prod")
                after(ve, "gated_hi", b, e)
                done(ve.tensor_tensor(gated[1][:, e, :], gate[:, e, :], f32(gated[0][:, e, :]), ALU.subtract), "gated_lo")

            def tail1(b, p):
                after(ve, "wo_ps", b, p)
                done(ve.tensor_tensor(x2[:, 2 * p:2 * p + 2, :], ps[:, 3 + p, :].rearrange("p (t n) -> p t n", t=2),
                                      bo_all[:, :].unsqueeze(1).to_broadcast([P, 2, D]), ALU.add), "x2")
                after(ve, "x2", b, p)
                normal_stats(1, b, p, lambda t: x2[:, t, :])
                if p == 1:
                    root_arg(1, b, 1.0, EPS)

            def tail2(b, p):
                after(ve, "rstd1", b)
                after(ve, "h_plus", b)
                for t in (2 * p, 2 * p + 1):
                    done(ve.scalar_tensor_tensor(x2[:, t, :], x2[:, t, :], mv[1][:, t, 0:1], ln2w_all[:, :],
                                                 ALU.subtract, ALU.mult), "t2")
                for t in (2 * p, 2 * p + 1):
                    after(ve, "t2", b, t)
                    done(ve.scalar_tensor_tensor(x2[:, t, :], x2[:, t, :], rstd[1][:, t:t + 1], h_plus[:, t, :],
                                                 ALU.mult, ALU.add), "h2")
                after(ve, "h2", b, 2 * p + 1)
                normal_stats(2, b, p, lambda t: x2[:, t, :])
                if p == 1:
                    root_arg(2, b, 1.0, EPS)

            def tail3(b, p):
                after(ve, "rstd2", b)
                after(ve, "tanh", b - 1)
                after(ve, "base", b - 1)
                for t in (2 * p, 2 * p + 1):
                    done(ve.tensor_scalar(y[:, t, :], x2[:, t, :], mv[2][:, t, 0:1], rstd[2][:, t:t + 1],
                                          ALU.subtract, ALU.mult), "y")
                for t in (2 * p, 2 * p + 1):
                    after(ve, "y", b, t)
                    item(ve, "score", b, t - 2)
                    done(ve.tensor_tensor_reduce(junk[:, half(t)], y[:, t, :], router_all[:, :], 1.0, 0.0,
                                                 ALU.mult, ALU.add, score[:, t:t + 1]), "score")

            def y_lo(b, p):
                after(ve, "y_hi", b, p)
                two = slice(2 * p, 2 * p + 2)
                done(ve.tensor_tensor(y_split[1][:, two, :], y[:, two, :], f32(y_split[0][:, two, :]),
                                      ALU.subtract), "y_lo")

            def ranks(b):
                after(ve, "srow_ps", b)
                for t in range(TILES):
                    s = score[:, t:t + 1]
                    if t >= 2:
                        after(ve, "count", b, (1, 4)[t - 2])
                    done(ve.tensor_scalar(junk8[:, SEQ * (t % 2) + P * t:SEQ * (t % 2) + SEQ], ps[:, 4, P * t:SEQ], s, 0.0, ALU.is_gt, ALU.add,
                                          accum_out=counts[:, t, 0:1]), "count")
                    if t:
                        done(ve.tensor_scalar(junk8[:, SEQ * (t % 2):SEQ * (t % 2) + P * t], ps[:, 4, 0:P * t], s, 0.0, ALU.is_ge, ALU.add,
                                              accum_out=counts[:, t, 1:2]), "count")
                    done(ve.scalar_tensor_tensor(junk8[:, 2 * SEQ + P * t:2 * SEQ + P * t + P], ps[:, 4, tok(t)], s, before[:, :], ALU.is_equal,
                                                 ALU.mult, accum_out=counts[:, t, 2:3]), "count")
                after(ve, "count", b)
                after(ve, "rrow_ps", b - 1)
                done(ve.tensor_reduce(rank[:, :], counts[:, :, :], AX.X, ALU.add), "rank")
                after(ve, "rank", b)
                after(ve, "ys_ps", b - 1)
                for t in range(TILES):
                    done(ve.tensor_scalar(pick[:, t, :], slots[:, :], rank[:, t:t + 1], None, ALU.is_equal), "pick")

            def make_weight(b):
                after(ve, "tanh", b)
                done(ve.tensor_scalar(weight[:, :], half_tanh[:, :], 0.5, 0.5, ALU.mult, ALU.add), "weight")

            for p in range(2):
                rows_lo(0, 2 * p)
                rows_lo(0, 2 * p + 1)
                h_stats(0, p)
            make_z(0, 0)
            make_z(0, 1)
            zT_lo(0, 0)
            zT_lo(0, 1)
            for i in range(2):
                ve.wait_ge(s_whi, 7 + i)
                part = (slice(None), bass.ts(i, FC // 2))
                ve.tensor_tensor(w_2[1][part], raw_2[i], f32(w_2[0][part]), ALU.subtract).then_inc(s_wlo, 1)
            ve.wait_ge(s_pool_set, 3)
            ve.wait_ge(s_rel, 16 * 2)

            def step(b, first=False, second=False, last=False):
                more = not last
                if not first and not second:
                    split_update(b - 2)
                if not first:
                    tail3(b - 1, 0)
                    tail3(b - 1, 1)
                    y_lo(b - 1, 0)
                    y_lo(b - 1, 1)
                rope(b, 0)
                if not first and not second:
                    result(b - 2)
                if not first:
                    ranks(b - 1)
                rope(b, 1)
                if not first:
                    take_rank_row(b - 1)
                    take_ys(b - 1)
                split_v(b, (0, 1))
                take_lk(b)
                split_v(b, (2, 3))
                take_quad(b)
                split_lq(b)
                split_kv(b)
                if not first:
                    split_hidden(b - 1, (0, 1))
                if more:
                    rows_lo(b + 1, 0)
                take_out(b, 0)
                if not first:
                    make_weight(b - 1)
                    split_hidden(b - 1, (2,))
                if more:
                    rows_lo(b + 1, 1)
                take_out(b, 1)
                if not first:
                    split_hidden(b - 1, (3,))
                if more:
                    rows_lo(b + 1, 2)
                take_out(b, 2)
                if more:
                    h_stats(b + 1, 0)
                    rows_lo(b + 1, 3)
                take_out(b, 3)
                if not first:
                    split_hidden(b - 1, (4, 5))
                if more:
                    h_stats(b + 1, 1)
                tail1(b, 0)
                if more:
                    make_z(b + 1, 0)
                tail1(b, 1)
                if not first:
                    split_hidden(b - 1, (6,))
                if more:
                    zT_lo(b + 1, 0)
                    make_z(b + 1, 1)
                tail2(b, 0)
                if not first:
                    split_hidden(b - 1, (7,))
                if more:
                    zT_lo(b + 1, 1)
                tail2(b, 1)

            step(0, first=True)
            step(1, second=True)
            with ve.Fori(2, BATCHES - 1) as b:
                step(b)
            step(BATCHES - 1, last=True)
            split_update(BATCHES - 2)
            tail3(BATCHES - 1, 0)
            tail3(BATCHES - 1, 1)
            y_lo(BATCHES - 1, 0)
            y_lo(BATCHES - 1, 1)
            result(BATCHES - 2)
            ranks(BATCHES - 1)
            make_weight(BATCHES - 1)
            take_rank_row(BATCHES - 1)
            take_ys(BATCHES - 1)
            split_hidden(BATCHES - 1, range(FC))
            split_update(BATCHES - 1)
            result(BATCHES - 1)

        @block.tensor
        def _(pe):
            pe.wait_ge(s_const, N_CONST)
            pe.wait_ge(s_stage["qk"], 16)
            pe.wait_ge(s_stage["v"], 16)
            pe.wait_ge(s_stage["g"], 16)
            for j in range(2):
                for c in range(DC):
                    m = pe.matmul(ps[:, 3, j:j + 1], raw_qk[:, c, j, :], ln1_b[:, c:c + 1], start=(c == 0), stop=(c == 1))
            m.then_inc(s_raw_used, 1)
            for e in range(HC):
                for c in range(DC):
                    m = pe.matmul(ps[:, 4, e:e + 1], raw_g[:, c, tok(e)], ln1_b[:, c:c + 1], start=(c == 0), stop=(c == 1))
            m.then_inc(s_raw_used, 1)
            for c in range(DC):
                m = pe.matmul(ps[0:1, 5, :], ln1_b[:, c:c + 1], raw_v[:, c, :], start=(c == 0), stop=(c == 1))
            m.then_inc(s_raw_used, 1)

            def rows_T(b, t):
                pe.wait_ge(gathered[t], (b + 1) * 16)
                if t == 0:
                    after(pe, "gate", b - 1)
                else:
                    after(pe, "rows_lo", b, t - 1)
                for c in range(EC):
                    m = pe.transpose(ps[:, 0, tok(c)], rows[:, t, tok(c)], ident[:, :])
                done(m, "rowsT_ps")

            def embed_mm(b, t):
                after(pe, "rows_lo", b, t)
                if t == 2:
                    after(pe, "h", b, 0)
                for c in range(EC):
                    m = mm3(pe, ps[:, 1, half(t)], both(rowsT, lambda x: x[:, t % 2, tok(c)]),
                            both(w_proj, lambda x: x[:, c, :]), c == 0, c == EC - 1)
                if t % 2:
                    done(m, "h_ps")

            def z_T(b, p):
                after(pe, "rows_lo", b)
                after(pe, "h", b)
                for t in (2 * p, 2 * p + 1):
                    after(pe, "z", b, t)
                    for c in range(DC):
                        m = pe.transpose(ps[:, t // 2, D * (t % 2) + P * c:D * (t % 2) + P * c + P],
                                         z[:, t % 2, tok(c)], ident[:, :])
                    done(m, "zT_ps")

            def qk(b):
                after(pe, "zT_lo", b)
                for j in range(2):
                    for c in range(DC):
                        m = mm3(pe, ps[:, j, :], both(w_qk, lambda x: x[:, c, j, :]),
                                both(zT, lambda x: x[:, c, :]), c == 0, c == 1)
                    done(m, "qk_ps")

            def vs(b, ts):
                after(pe, "prod", b - 1)
                after(pe, "x2", b - 1, 0)
                for t in ts:
                    if t >= 2:
                        after(pe, "v", b, t - 2)
                    pe.matmul(ps[:, 2 + t % 2, :], ones[:, :], bv_rows[:, :], start=True, stop=False)
                    for c in range(DC):
                        m = mm3(pe, ps[:, 2 + t % 2, :], both(zT, lambda x: x[:, c, tok(t)]),
                                both(w_v, lambda x: x[:, c, :]), False, c == 1)
                    done(m, "v_ps")

            def gates(b, e):
                if e < 2:
                    after(pe, "qk", b, e)
                else:
                    after(pe, "gate", b, e - 2)
                for c in range(DC):
                    m = mm3(pe, ps[:, e % 2, :], both(w_g, lambda x: x[:, c, tok(e)]),
                            both(zT, lambda x: x[:, c, :]), c == 0, c == 1)
                done(m, "gate_ps")

            def rank_row(b):
                after(pe, "rank", b)
                for t in range(TILES):
                    m = pe.transpose(ps[:, 4, tok(t)], rank[:, t:t + 1].to_broadcast([P, P]), ident[:, :])
                done(m, "rrow_ps")

            def select(b):
                after(pe, "pick", b)
                after(pe, "y_lo", b)
                after(pe, "upd", b - 1)
                after(pe, "res", b - 1)
                for c in range(DC):
                    for part in range(2):
                        for t in range(TILES):
                            m = pe.matmul(ps[:, 6 + part, TOP * c:TOP * c + TOP], y_split[part][:, t, tok(c)],
                                          pick[:, t, :], start=(t == 0), stop=(t == TILES - 1))
                done(m, "ys_ps")

            def ff1(b, g):
                if g == 0:
                    after(pe, "ys_hi", b)
                    after(pe, "ys_lo", b)
                if g >= 2:
                    after(pe, "act", b, 2 * g - 3)
                for f in (2 * g, 2 * g + 1):
                    for c in range(DC):
                        m = mm3(pe, ps[:, 5 + 2 * (g % 2), half(f)], both(w_1, lambda x: x[:, c, tok(f)]),
                                both(ys, lambda x: x[:, c, :]), c == 0, c == 1)
                done(m, "ff1_ps")

            def ff2(b, f):
                after(pe, "hid_lo", b, f)
                for k in range(2):
                    for i, j in ((0, 0), (1, 0), (0, 1)):
                        m = pe.matmul(ps[:, 6, half(k)], hid[i][:, f % RING, tok(k)], w_2[j][:, f, :],
                                      start=(f == 0 and k == 0 and i + j == 0), stop=(f == FC - 1 and j == 1),
                                      skip_group_check=True)
                done(m, "ff2_ps")

            def put_back(b):
                after(pe, "upd_lo", b)
                after(pe, "put", b)
                after(pe, "act", b)
                for t in range(TILES):
                    n = 0
                    for k in range(2):
                        for part in range(2):
                            m = pe.matmul(ps[:, 5 + 2 * (t // 2), half(t)], put[:, k, tok(t)], updp[part][:, k, :],
                                          start=(n == 0), stop=(n == 3))
                            n += 1
                    if t % 2:
                        done(m, "put_ps")

            def quad(b):
                after(pe, "put", b - 1)
                after(pe, "rope", b)
                after(pe, "v", b, 2)
                for t in range(TILES):
                    m = pe.matmul(ps[:, 2, tok(t)], heads[QK:P, 1, tok(t)], heads[QK:P, 0, tok(t)],
                                  start=True, stop=True)
                done(m, "quad_ps")
                for t in range(TILES):
                    m = pe.transpose(ps[:, 4, QK * t:QK * t + QK], heads[0:QK, 1, tok(t)], ident[0:QK, 0:QK])
                done(m, "lkT_ps")

            def kvs(b):
                after(pe, "v", b, 3)
                after(pe, "lk_lo", b)
                for t in range(TILES):
                    after(pe, "v_lo", b, t)
                    m = mm3(pe, ps[0:QK, 3, :], both(lk, lambda x: x[:, t, :]),
                            both(v_split, lambda x: x[:, t, :]), t == 0, t == TILES - 1)
                    done(m, "kv_ps")

            def outs(b, e):
                bank = 4 if e % 2 == 0 else 2
                if e == 0:
                    after(pe, "kv_lo", b)
                    after(pe, "lq_lo", b)
                    after(pe, "attn", b)
                if e >= 2:
                    after(pe, "prod", b, e - 2)
                mm3(pe, ps[:, bank, :], both(kv, lambda x: x[:, tok(e)]), both(lq, lambda x: x[:, :]), True, False, shared=True)
                for t in range(TILES):
                    m = pe.matmul(ps[:, bank, tok(t)], v[:, t, tok(e)], attnT[:, t, :],
                                  start=False, stop=True, skip_group_check=True)
                done(m, "out_ps")

            def project(b):
                after(pe, "gated_lo", b)
                for t in range(TILES):
                    for e in range(HC):
                        m = mm3(pe, ps[:, 3 + t // 2, half(t)], both(gated, lambda x: x[:, e, tok(t)]),
                                both(w_o, lambda x: x[:, e, :]), e == 0, e == HC - 1)
                    if t % 2:
                        done(m, "wo_ps")

            def score_row(b):
                after(pe, "score", b)
                after(pe, "x2", b)
                for t in range(TILES):
                    m = pe.transpose(ps[:, 4, tok(t)], score[:, t:t + 1].to_broadcast([P, P]), ident[:, :])
                done(m, "srow_ps")

            pe.wait_ge(s_wlo, 1)
            pe.wait_ge(s_set, 6)
            pe.wait_ge(s_pool_set, 3)
            pe.wait_ge(s_bias, 5)
            rows_T(0, 0)
            embed_mm(0, 0)
            for t in range(1, TILES):
                rows_T(0, t)
                embed_mm(0, t)
            z_T(0, 0)
            z_T(0, 1)
            pe.wait_ge(s_wlo, N_SPLIT)

            def step(b, first=False, second=False, last=False):
                more = not last
                qk(b)
                if not first and not second:
                    put_back(b - 2)
                vs(b, (0, 1))
                if not first:
                    score_row(b - 1)
                vs(b, (2, 3))
                gates(b, 0)
                gates(b, 1)
                if not first:
                    rank_row(b - 1)
                    select(b - 1)
                gates(b, 2)
                quad(b)
                gates(b, 3)
                kvs(b)
                if not first:
                    ff1(b - 1, 0)
                if more:
                    rows_T(b + 1, 0)
                outs(b, 0)
                if not first:
                    ff1(b - 1, 1)
                if more:
                    embed_mm(b + 1, 0)
                    rows_T(b + 1, 1)
                outs(b, 1)
                if not first:
                    ff2(b - 1, 0)
                if more:
                    embed_mm(b + 1, 1)
                    rows_T(b + 1, 2)
                outs(b, 2)
                if not first:
                    ff2(b - 1, 1)
                if more:
                    embed_mm(b + 1, 2)
                    rows_T(b + 1, 3)
                outs(b, 3)
                if not first:
                    ff2(b - 1, 2)
                    ff1(b - 1, 2)
                if more:
                    embed_mm(b + 1, 3)
                project(b)
                if not first:
                    ff2(b - 1, 3)
                    ff1(b - 1, 3)
                if more:
                    z_T(b + 1, 0)
                if not first:
                    ff2(b - 1, 4)
                    ff2(b - 1, 5)
                if more:
                    z_T(b + 1, 1)
                if not first:
                    ff2(b - 1, 6)
                    ff2(b - 1, 7)

            step(0, first=True)
            step(1, second=True)
            with pe.Fori(2, BATCHES - 1) as b:
                step(b)
            step(BATCHES - 1, last=True)
            put_back(BATCHES - 2)
            score_row(BATCHES - 1)
            rank_row(BATCHES - 1)
            select(BATCHES - 1)
            ff1(BATCHES - 1, 0)
            ff1(BATCHES - 1, 1)
            for g in range(FC // 2):
                ff2(BATCHES - 1, 2 * g)
                ff2(BATCHES - 1, 2 * g + 1)
                if g < 2:
                    ff1(BATCHES - 1, g + 2)
            put_back(BATCHES - 1)


def constants():
    half = QK // 2
    inv = (np.float32(10000.0) ** (-np.arange(half, dtype=np.float32) / np.float32(half))).astype(np.float32)
    ang = (np.arange(SEQ, dtype=np.float32)[:, None] * inv[None, :]).astype(np.float32)
    sin, cos = np.sin(ang).T, np.cos(ang).T
    return {
        "cos": np.concatenate([cos] * 4).astype(np.float32),
        "sin": np.concatenate([-sin, sin] * 2).astype(np.float32),
        "ident": np.eye(P, dtype=np.float32),
        "before": (np.arange(P)[None, :] < np.arange(P)[:, None]).astype(np.float32),
        "slots": np.tile(np.arange(TOP, dtype=np.float32), (P, 1)),
        "slot_of": (np.arange(P)[:, None] + P * np.arange(2)[None, :]).astype(np.float32),
    }


def kernel(**inputs):
    import concourse.bacc as bacc
    from concourse.bass_utils import run_bass_kernel_spmd

    g = {k: np.asarray(x) for k, x in inputs.items()}
    table = np.zeros((VOCAB + 1, ROW), np.float32)
    proj = np.zeros((EC * P, D), np.float32)
    row = col = 0
    for i, w in enumerate(WIDTHS):
        emb = g[f"L0_tok_emb_{i}"]
        table[row:row + emb.shape[0], col:col + w] = emb
        proj[col:col + w] = g[f"L0_tok_proj_{i}"].T
        row, col = row + emb.shape[0], col + w

    def rows_of(w, chunks):
        return np.ascontiguousarray(w.reshape(chunks, P, -1).transpose(1, 0, 2))

    def column(x, n):
        return np.ascontiguousarray(x.reshape(n, P).T)

    def swap(x):
        return np.concatenate([x[QK // 2:], x[:QK // 2]])

    wqk = g["L0_attn_Wqk"]
    wqk2 = np.concatenate([wqk, wqk, swap(wqk), swap(wqk)])

    def by_head(x):
        q, lq, k, lk = x
        cols = []
        for lin, quad in ((lq, q), (lk, k)):
            cols += [np.concatenate([lin, quad]), np.concatenate([swap(lin), swap(quad)])]
        return np.ascontiguousarray(np.stack(cols, 1))

    bqk = g["L0_attn_bqk"]
    arrays = {
        "ids": np.ascontiguousarray(g["x"].reshape(-1, P).T),
        "table": table,
        "w_proj": rows_of(proj, EC),
        "w_qk": np.ascontiguousarray(wqk2.T.reshape(DC, P, 2, P).transpose(1, 0, 2, 3)),
        "w_v": rows_of(g["L0_attn_Wv"].T, DC),
        "w_g": rows_of(g["L0_attn_Wg"].T, DC),
        "w_o": rows_of(g["L0_attn_Wo"].T, HC),
        "w_w1": rows_of(g["L0_ffn_W1"], DC),
        "w_w2": rows_of(g["L0_ffn_W2"], FC),
        "ln1_w": column(g["L0_attn_ln1_w"], DC),
        "ln1_b": column(g["L0_attn_ln1_b"], DC),
        "b_qk": column(np.concatenate([bqk, bqk, swap(bqk), swap(bqk)]), 2),
        "b_v": g["L0_attn_bv"].reshape(1, H),
        "b_g": column(g["L0_attn_bg"], HC),
        "b_1": column(g["L0_ffn_b1"], FC),
        "b_o": g["L0_attn_bo"],
        "b_2": g["L0_ffn_b2"],
        "ln2_w": g["L0_attn_ln2_w"],
        "ln2_b": g["L0_attn_ln2_b"],
        "router": g["L0_ffn_w_router"],
        "head_gain": by_head(g["L0_attn_gamma"]),
        "head_bias": by_head(g["L0_attn_beta"]),
        "pos": g["L0_attn_pos_emb"][:MAX_REL + 1].reshape(1, -1),
        **constants(),
    }
    nc = bacc.Bacc("TRN2", target_bir_lowering=False, num_devices=1)
    aps = {k: nc.dram_tensor("in_" + k, x.shape, mybir.dt.from_np(x.dtype), kind="ExternalInput").ap()
           for k, x in arrays.items()}
    out = nc.dram_tensor("out_0", (BATCHES * SEQ, D), F32, kind="ExternalOutput").ap()
    build(nc, aps, out)
    r = run_bass_kernel_spmd(nc, [{"in_" + k: x for k, x in arrays.items()}], core_ids=[0])
    return r.results[0]["out_0"].reshape(BATCHES, SEQ, D)
```

```python
from contextlib import ExitStack

import numpy as np
import concourse.bass as bass
from concourse import mybir

ALU = mybir.AluOpType
ACT = mybir.ActivationFunctionType
AX = mybir.AxisListType
F32 = mybir.dt.float32
F32R = mybir.dt.float32r
I32 = mybir.dt.int32

P = 128
BATCHES, SEQ = 16, 512
TILES = SEQ // P
VOCAB = 32000
WIDTHS = (256, 64, 16, 4)
ROW = sum(WIDTHS)
EC = 3
D, DC = 256, 2
QK, GROUP, MAX_REL = 64, 64, 32
H, HC = 512, 4
F, FC = 1024, 8
TOP = 256
EPS = 1e-5
RING = 3
LATE = [("before", P), ("slots", TOP), ("cos", SEQ), ("sin", SEQ)]
COLUMNS = [("ident", P), ("slot_of", 2), ("head_gain", 4), ("head_bias", 4), ("ln1_w", DC), ("ln1_b", DC),
           ("b_qk", 1), ("b_g", HC), ("b_1", FC)] + LATE


def build(nc, a, out):
    ctx = ExitStack()
    with ctx:
        def sb(name, shape, dt=F32):
            return ctx.enter_context(nc.sbuf_tensor(name, shape, dt))

        def sem(name):
            return ctx.enter_context(nc.semaphore(name))

        def pair(name, shape):
            return (sb(name + "_hi", shape, F32R), sb(name + "_lo", shape, F32R))

        w_proj = pair("w_proj", [P, EC, D])
        w_qk = pair("w_qk", [P, DC, P])
        w_v = pair("w_v", [P, DC, H])
        w_g = pair("w_g", [P, DC, H])
        w_o = pair("w_o", [P, HC, D])
        w_1 = pair("w_1", [P, DC, F])
        w_2 = pair("w_2", [P, FC, D])
        cols = {}
        n = 0
        for name, width in COLUMNS:
            cols[name] = slice(n, n + width)
            n += width
        early = sb("early", [P, n - sum(w for _, w in LATE)])
        late = sb("late", [P, sum(w for _, w in LATE)])

        def const(name):
            c = cols[name]
            k = early.shape[1]
            return early[:, c] if c.stop <= k else late[:, c.start - k:c.stop - k]

        ident, slot_of, head_gain, head_bias, ln1_w, ln1_b, b_qk, b_g, b_1, before, slots, cos, sin = (
            const(name) for name, _ in COLUMNS)
        rel_bias = sb("rel_bias", [P, GROUP])
        table_probe = sb("table_probe", [1, 2])
        rel_row = sb("rel_row", [1, 2 * GROUP])
        pos_row = sb("pos_row", [1, MAX_REL + 1])
        bv_rows, bo_rows, b2_rows = (sb(name, [P, 512], F32R) for name in ("bv_rows", "bo_rows", "b2_rows"))
        ones = sb("ones", [P, P], F32R)
        all_rows = sb("all_rows", [P, 3, D])
        ln2w_all, ln2b_all, router_all = (all_rows[:, i, :] for i in range(3))
        neg_half = sb("neg_half", [P, TILES])
        ids = sb("ids", [P, (BATCHES + 1) * TILES], I32)
        ids_now = sb("ids_now", [P, TILES], I32)
        rows = sb("rows", [P, TILES, EC * P])
        rowsT = pair("rowsT", [P, 2, EC * P])
        h = sb("h", [P, TILES, D])
        h_plus = sb("h_plus", [P, TILES, D])
        z = sb("z", [P, 2, D])
        zT = pair("zT", [P, DC, SEQ])
        stats = [sb(f"stats{i}", [P, TILES, 6]) for i in range(3)]
        mv = [sb(f"mv{i}", [P, TILES, 2]) for i in range(3)]
        arg = [sb(f"arg{i}", [P, TILES]) for i in range(3)]
        rstd = [sb(f"rstd{i}", [P, TILES]) for i in range(3)]
        neg_mean = [sb(f"neg_mean{i}", [P, TILES]) for i in range(3)]
        shift = [sb(f"shift{i}", [P, TILES]) for i in range(3)]
        gate = sb("gate", [P, HC, SEQ])
        qk_act = gate[:, 0:2, :]
        x2 = gate[:, 2:4, :].rearrange("p a (b d) -> p (a b) d", d=D)
        scaled = sb("scaled", [P, 2, SEQ])
        heads = sb("heads", [P, 2, SEQ])
        lk = sb("lk", [P, TILES, 2, QK], F32R)
        v = sb("v", [P, TILES, H])
        y_split = pair("y_split", [P, TILES, D])
        attnT = sb("attnT", [P, TILES, P])
        kv = [sb(name, [P, H], F32R) for name in ("kv_hi_hi", "kv_lo_hi")]
        lq = [sb(name, [P, SEQ], F32R) for name in ("lq_hi_hi", "lq_hi_lo")]
        v_or_gated = pair("v_or_gated", [P, HC, SEQ])
        v_split = gated = v_or_gated
        y = sb("y", [P, TILES, D])
        base = sb("base", [P, TILES, D])
        junk = sb("junk", [P, SEQ])
        junk8 = junk[:, :].bitcast(mybir.dt.uint8)
        pre = junk[:, 0:TILES * GROUP].rearrange("p (t x) -> p t x", x=GROUP)
        score = sb("score", [P, TILES])
        counts = sb("counts", [P, TILES, 3])
        rank = sb("rank", [P, TILES])
        pick = sb("pick", [P, TILES, TOP], F32R)
        half_tanh = sb("half_tanh", [P, TILES])
        weight = sb("weight", [P, TILES])
        put = sb("put", [P, 2, SEQ], F32R)
        ys = pair("ys", [P, DC, TOP])
        act = sb("act", [P, 2, TOP])
        hid = pair("hid", [P, RING, TOP])
        updp = ys
        ob = sb("ob", [P, TILES, D])

        ps = ctx.enter_context(nc.psum_tensor("ps", [P, 8, 512], F32))
        rel_dram = nc.dram_tensor("rel_scratch", [GROUP, 2 * GROUP], F32, kind="Internal").ap()

        PER = {}

        def S(name, per):
            PER[name] = per
            return name

        sems = {}
        for name, per in dict(
            rowsT_ps=4, rows_hi=4, rows_lo=4, h_ps=2, h=2, h_plus=1,
            stat0=4, mv0=4, arg0=1, rstd0=1, shift0=1, stat1=4, mv1=4, arg1=1, rstd1=1,
            stat2=4, mv2=4, arg2=1, rstd2=1, shift2=1,
            z=4, zT_ps=4, zT_hi=2, zT_lo=2,
            qk_ps=1, qk=3, scaled=4, rope=6, lq_hi=3, lq_lo=1,
            v_ps=4, v=4, v_hi=4, v_lo=4, gate_ps=4, gate=4,
            lkT_ps=1, lk_hi=1, lk_lo=1, quad_ps=1, pre=2, attn=2,
            kv_ps=4, kv_hi=2, kv_lo=1, out_ps=4, prod=4, gated_hi=4, gated_lo=4,
            wo_ps=2, t2=4, h2=4, y=4, y_hi=2, y_lo=2, score=4, base=4,
            srow_ps=1, count=11, rank=1, pick=4, tanh=1, weight=1,
            rrow_ps=1, put=2, ys_ps=1, ys_hi=1, ys_lo=1,
            ff1_ps=4, act=8, hid_hi=8, hid_lo=8, ff2_ps=8, upd_hi=1, upd_lo=1,
            put_ps=2, res=4, stored=1, ids=1,
        ).items():
            PER[name] = per
            sems[name] = sem("s_" + name)
        gathered = [sem(f"s_gathered{t}") for t in range(TILES)]
        s_const = sem("s_const")
        s_pos = sem("s_pos")
        s_ids = sem("s_loaded_ids")
        s_early = sem("s_early")
        s_rel_row = sem("s_rel_row")
        s_rel_dram = sem("s_rel_dram")
        s_rel = sem("s_rel")
        s_cast = sem("s_cast")
        s_pool_set = sem("s_pool_set")
        s_set = sem("s_set")
        s_stage = {k: sem("s_stage_" + k) for k in ("proj", "qk", "v", "g", "o", "w1", "w2")}
        s_raw_used = sem("s_raw_used")
        s_scaled = sem("s_wscaled")
        s_bias = sem("s_bias")
        s_whi = sem("s_whi")
        s_wlo = sem("s_wlo")

        def after(eng, name, b, k=None):
            per = PER[name]
            k = per - 1 if k is None else k
            if isinstance(b, int) and b < 0:
                return
            eng.wait_ge(sems[name], b * per + (k + 1))

        def item(eng, name, b, k):
            per = PER[name]
            if k < 0:
                after(eng, name, b - 1, k + per)
            else:
                after(eng, name, b, k)

        def after_apart(eng, *items):
            waits = []
            for name, b, k in items:
                if k < 0:
                    b, k = b - 1, k + PER[name]
                if isinstance(b, int) and b < 0:
                    continue
                value = b * PER[name] + (k + 1)
                waits.append((name, value if isinstance(b, int) else eng.snap(value)))
            eng.wait_ge(s_early, 16)
            for name, value in waits:
                eng.wait_ge(sems[name], value)

        def done(ins, name):
            ins.then_inc(sems[name], 1)

        def f32(ap):
            return ap.bitcast(F32)

        def mm3(eng, o, lhs, rhs, start, stop, shared=False):
            eng.matmul(o, lhs[0], rhs[0], start=start, stop=False, skip_group_check=shared)
            eng.matmul(o, lhs[1], rhs[0], start=False, stop=False, skip_group_check=shared)
            return eng.matmul(o, lhs[0], rhs[1], start=False, stop=stop, skip_group_check=shared)

        def both(p, f):
            return f(p[0]), f(p[1])

        def tok(t):
            return slice(P * t, P * t + P)

        def half(t):
            return slice(D * (t % 2), D * (t % 2) + D)

        raw_proj = gate[:, 0:2, :].rearrange("p a n -> p (a n)")[:, 0:EC * D].rearrange("p (c n) -> p c n", c=EC)
        raw_qk = act[:, :, :].rearrange("p a n -> p (a n)")[:, 0:DC * P].rearrange("p (c n) -> p c n", c=DC)
        raw_v = v[:, 0:2, :]
        raw_g = v[:, 2:4, :]
        raw_o = ob[:, :, :]
        raw_1 = [x[:, :, :].rearrange("p (c a) n -> p c (a n)", c=1) for x in (base, y)]
        raw_2 = [x[:, :, :] for x in (base, y)]
        bv_raw = junk[0:1, :]
        bo_raw, b2_raw = (h_plus[0:1, i:i + 2, :].rearrange("p a n -> p (a n)") for i in (0, 2))
        SPLIT = dict(proj=1, qk=2, v=3, g=4, o=5, w1=7, w2=9)

        N_CONST = 16 * 5

        block = ctx.enter_context(nc.Block())

        @block.sync
        def _(sp):
            sp.dma_start(ids[:, 0:BATCHES * TILES], a["ids"]).then_inc(s_ids, 16)
            sp.dma_start(raw_proj, a["w_proj"]).then_inc(s_stage["proj"], 16)
            sp.dma_start(early[:, :], a["early"]).then_inc(s_early, 16)
            sp.dma_start(pos_row[:, :], a["pos"]).then_inc(s_pos, 16)
            sp.dma_start(raw_qk, a["w_qk"]).then_inc(s_stage["qk"], 16)
            for dst, src in ((bv_raw, "b_v"), (bo_raw, "b_o"), (b2_raw, "b_2")):
                sp.dma_start(dst, a[src]).then_inc(s_const, 16)
            sp.dma_start(raw_v, a["w_v"]).then_inc(s_stage["v"], 16)
            sp.dma_start(raw_g, a["w_g"]).then_inc(s_stage["g"], 16)
            sp.dma_start(all_rows[:, :, :].rearrange("p a n -> p (a n)"), a["rows"].partition_broadcast(P)).then_inc(s_const, 16)
            sp.dma_start(late[:, :], a["late"]).then_inc(s_const, 16)
            sp.dma_start(raw_o, a["w_o"]).then_inc(s_stage["o"], 16)
            for c in range(DC):
                sp.dma_start(raw_1[c], a["w_w1"][:, c:c + 1, :]).then_inc(s_stage["w1"], 16)
            sp.wait_ge(s_rel_row, 3)
            sp.dma_start(rel_dram, rel_row[0:1, :].unsqueeze(1).to_broadcast([1, GROUP, 2 * GROUP])).then_inc(s_rel_dram, 16)
            sp.wait_ge(s_rel_dram, 16)
            for g in range(2):
                rows_back = bass.AP(rel_dram.tensor, GROUP - 1, [[2 * GROUP - 1, GROUP], [1, GROUP]])
                sp.dma_start(rel_bias[GROUP * g:GROUP * g + GROUP, :], rows_back).then_inc(s_rel, 16)
            sp.wait_ge(s_wlo, SPLIT["w1"])
            for i in range(2):
                sp.dma_start(raw_2[i], a["w_w2"][:, bass.ts(i, FC // 2), :]).then_inc(s_stage["w2"], 16)

            with sp.Fori(0, BATCHES) as b:
                after(sp, "res", b)
                sp.dma_start(out[bass.ds(b * SEQ, SEQ), :].rearrange("(t p) d -> p t d", p=P), ob[:, :, :]
                             ).then_inc(sems["stored"], 16)
            sp.wait_ge(sems["stored"], 16 * BATCHES)

        @block.gpsimd
        def _(pool):
            pool.memset(neg_half[:, :], -0.5).then_inc(s_pool_set, 1)
            pool.memset(table_probe[:, :], 0.0).then_inc(s_pool_set, 1)
            pool.memset(rows[:, :, :], 0.0).then_inc(s_pool_set, 1)
            pool.memset(attnT[:, :, :], 0.0).then_inc(s_pool_set, 1)
            pool.wait_ge(s_cast, 1)
            pool.wait_ge(s_pool_set, 4)

            def gather(b, between=None):
                if not (isinstance(b, int) and b == 0):
                    for t in range(TILES):
                        pool.wait_ge(gathered[t], 16 * b)
                    after(pool, "rowsT_ps", b - 1)
                done(pool.tensor_copy(ids_now[:, :], ids[:, bass.ds(b * TILES, TILES)]), "ids")
                after(pool, "ids", b)
                if between:
                    between()
                for t in range(TILES):
                    pool.indirect_dma_start(
                        rows[:, t, 0:ROW], None, a["table"],
                        bass.IndirectOffsetOnAxis(ap=ids_now[:, t:t + 1].bitcast(mybir.dt.uint32), axis=0),
                    ).then_inc(gathered[t], 16)

            def root(i, b):
                after(pool, f"arg{i}", b)
                after(pool, ("z", "h2", "y")[i], b - 1)
                done(pool.tensor_tensor(rstd[i][:, :], arg[i][:, :], neg_half[:, :], ALU.pow), f"rstd{i}")
                if i != 1:
                    after(pool, f"rstd{i}", b)
                    done(pool.tensor_tensor(shift[i][:, :], neg_mean[i][:, :], rstd[i][:, :], ALU.mult), f"shift{i}")

            def add_ln2b(b):
                after(pool, "h", b)
                after(pool, "h2", b - 1)
                done(pool.tensor_tensor(h_plus[:, :, :], h[:, :, :],
                                        ln2b_all.unsqueeze(1).to_broadcast([P, TILES, D]), ALU.add), "h_plus")

            def add_base(b):
                after(pool, "res", b - 1)
                for t in range(TILES):
                    after(pool, "y", b, t)
                    done(pool.tensor_tensor(base[:, t, :], x2[:, t, :], y[:, t, :], ALU.add), "base")

            def split_v(b, ts):
                after(pool, "wo_ps", b - 1)
                for t in ts:
                    after(pool, "v_hi", b, t)
                    done(pool.tensor_tensor(v_split[1][:, t, :], v[:, t, :], f32(v_split[0][:, t, :]),
                                            ALU.subtract), "v_lo")

            def split_y(b):
                after(pool, "ys_ps", b - 1)
                for p in range(2):
                    after(pool, "y_hi", b, p)
                    two = slice(2 * p, 2 * p + 2)
                    done(pool.tensor_tensor(y_split[1][:, two, :], y[:, two, :], f32(y_split[0][:, two, :]),
                                            ALU.subtract), "y_lo")

            gather(0)
            root(0, 0)
            gather(1)
            pool.wait_ge(s_const, N_CONST)

            def step(b, first=False, last=False):
                if not first:
                    root(2, b - 1)
                split_v(b, (0, 1))
                if not first:
                    add_base(b - 1)
                split_v(b, (2, 3))
                if first:
                    pool.wait_ge(s_bias, 9)
                if not first:
                    split_y(b - 1)
                add_ln2b(b)

                def roots():
                    root(0, b + 1)
                    root(1, b)

                if last:
                    root(1, b)
                else:
                    gather(b + 2, roots)

            step(0, first=True)
            step(1)
            with pool.Fori(2, BATCHES - 1) as b:
                step(b)
            step(BATCHES - 1, last=True)
            root(2, BATCHES - 1)
            add_base(BATCHES - 1)
            split_y(BATCHES - 1)

        @block.scalar
        def _(sc):
            def split_hi(k, w, raw):
                if k in ("qk", "v", "g"):
                    sc.wait_ge(s_scaled, DC * (1 + ("qk", "v", "g").index(k)))
                sc.wait_ge(s_stage[k], 16)
                sc.activation(w[0][:, :, :], raw, ACT.Copy).then_inc(s_whi, 1)

            def rows_hi(b, t):
                after(sc, "rowsT_ps", b, t)
                if t < 2:
                    after(sc, "h_ps", b - 1)
                else:
                    after(sc, "h_ps", b, 0)
                done(sc.activation(rowsT[0][:, t % 2, :], ps[:, 0, 0:EC * P], ACT.Copy), "rows_hi")

            def switch_table(function):
                sc.activation(table_probe[:, 1:2], table_probe[:, 0:1], function)

            def take_h(b, p):
                after(sc, "h_ps", b, p)
                after(sc, "z", b - 1)
                after(sc, "h_plus", b - 1)
                done(sc.activation(h[:, 2 * p:2 * p + 2, :], ps[:, 1, :].rearrange("p (t n) -> p t n", t=2),
                                   ACT.Copy, scale=float(D ** 0.5)), "h")

            def make_z(b, p):
                after(sc, "shift0", b)
                for t in (2 * p, 2 * p + 1):
                    item(sc, "zT_ps", b, t - 2)
                    done(sc.activation(z[:, t % 2, :], h[:, t, :], ACT.Identity, bias=shift[0][:, t:t + 1],
                                       scale=rstd[0][:, t:t + 1]), "z")

            def make_y(b, p):
                after(sc, "shift2", b)
                after(sc, "base", b - 1)
                after(sc, "y_lo", b - 1)
                after(sc, "score", b - 1)
                for t in (2 * p, 2 * p + 1):
                    done(sc.activation(y[:, t, :], x2[:, t, :], ACT.Identity, bias=shift[2][:, t:t + 1],
                                       scale=rstd[2][:, t:t + 1]), "y")

            def zT_hi(b, p):
                after(sc, "zT_ps", b, 2 * p + 1)
                after(sc, "gate_ps", b - 1)
                done(sc.activation(
                    zT[0][:, :, D * p:D * p + D].rearrange("p c (t x) -> p t c x", x=P),
                    ps[:, p, :].rearrange("p (t c x) -> p t c x", t=2, c=DC), ACT.Copy), "zT_hi")

            def take_qk(b):
                after(sc, "qk_ps", b)
                after(sc, "gated_lo", b - 1)
                done(sc.activation(qk_act[:, 0, :], ps[:, 0, :], ACT.Silu, bias=b_qk), "qk")
                for here, there in ((slice(0, QK), slice(QK, P)), (slice(QK, P), slice(0, QK))):
                    done(sc.activation(qk_act[here, 1, :], ps[there, 0, :], ACT.Silu, bias=b_qk[there, :]), "qk")

            def scale_heads(b, p):
                for j in range(2):
                    if p == 0:
                        after(sc, "qk", b, 2 * j)
                        after(sc, "rope", b - 1)
                    else:
                        after(sc, "rope", b, 2 if j else 0)
                    done(sc.activation(scaled[:, j, :], qk_act[:, j, :], ACT.Identity,
                                       bias=head_bias[:, 2 * p + j:2 * p + j + 1],
                                       scale=head_gain[:, 2 * p + j:2 * p + j + 1]), "scaled")

            def take_v(b, ts):
                for t in ts:
                    after(sc, "v_ps", b, t)
                    after(sc, "out_ps", b - 1)
                    done(sc.activation(v[:, t, :], ps[:, 2 + t % 2, :], ACT.Silu), "v")

            def take_gate(b, e):
                after(sc, "gate_ps", b, e)
                if e < 2:
                    after(sc, "scaled", b)
                else:
                    after(sc, "base", b - 1)
                done(sc.activation(gate[:, e, :], ps[:, e % 2, :], ACT.Silu, bias=b_g[:, e:e + 1]), "gate")

            def take_ys(b):
                after(sc, "ys_ps", b)
                done(sc.activation(ys[0][:, :, :], ps[:, 6, :].rearrange("p (c n) -> p c n", c=DC), ACT.Copy), "ys_hi")

            def y_hi(b, p):
                after(sc, "y", b, 2 * p + 1)
                after(sc, "ys_ps", b - 1)
                done(sc.activation(y_split[0][:, 2 * p:2 * p + 2, :], y[:, 2 * p:2 * p + 2, :], ACT.Copy), "y_hi")

            def upd_hi(b):
                after(sc, "ff2_ps", b)
                done(sc.activation(updp[0][:, :, :], ps[:, 6, :].rearrange("p (k n) -> p k n", k=2), ACT.Copy), "upd_hi")

            def gelu(b, f):
                after(sc, "ff1_ps", b, f // 2)
                item(sc, "hid_lo", b, f - 2)
                item(sc, "hid_hi", b, f - 2)
                done(sc.activation(act[:, f % 2, :], ps[:, 5 + 2 * (f // 2 % 2), half(f)], ACT.Gelu_apprx_tanh,
                                   bias=b_1[:, f:f + 1]), "act")
                after(sc, "act", b, f)
                item(sc, "ff2_ps", b, f - RING)
                done(sc.activation(hid[0][:, f % RING, :], act[:, f % 2, :], ACT.Copy), "hid_hi")

            def take_lk(b):
                after(sc, "lkT_ps", b)
                after(sc, "kv_ps", b - 1)
                done(sc.activation(lk[:, :, 0, :], ps[:, 3, 0:TILES * QK].rearrange("p (t c) -> p t c", c=QK),
                                   ACT.Copy), "lk_hi")

            def v_hi(b, ts):
                for t in ts:
                    after(sc, "v", b, t)
                    after(sc, "wo_ps", b - 1)
                    done(sc.activation(v_split[0][:, t, :], v[:, t, :], ACT.Copy), "v_hi")

            def gated_hi(b, e):
                after(sc, "prod", b, e)
                after(sc, "kv_ps", b)
                done(sc.activation(gated[0][:, e, :], gate[:, e, :], ACT.Copy), "gated_hi")

            def lq_hi(b):
                after(sc, "rope", b, 2)
                after(sc, "out_ps", b - 1)
                for o in (lq[0][0:QK, :], lq[0][QK:P, :], lq[1][0:QK, :]):
                    done(sc.activation(o, heads[0:QK, 0, :], ACT.Copy), "lq_hi")

            def take_kv(b):
                after(sc, "kv_ps", b)
                after(sc, "out_ps", b - 1)
                done(sc.activation(kv[0][:, :], ps[:, 3, :], ACT.Copy), "kv_hi")
                done(sc.activation(kv[1][QK:P, :], ps[0:QK, 3, :], ACT.Copy), "kv_hi")

            def router_tanh(b):
                after(sc, "score", b)
                after(sc, "weight", b - 1)
                done(sc.activation(half_tanh[:, :], score[:, :], ACT.Tanh, scale=0.5), "tanh")

            sc.wait_ge(s_pool_set, 4)
            split_hi("proj", w_proj, raw_proj)
            rows_hi(0, 0)
            rows_hi(0, 1)
            take_h(0, 0)
            split_hi("qk", w_qk, raw_qk)
            rows_hi(0, 2)
            rows_hi(0, 3)
            take_h(0, 1)
            switch_table(ACT.Silu)
            make_z(0, 0)
            make_z(0, 1)
            zT_hi(0, 0)
            zT_hi(0, 1)
            split_hi("v", w_v, raw_v)
            split_hi("g", w_g, raw_g)
            sc.wait_ge(s_const, N_CONST)
            sc.wait_ge(s_bias, 3)

            def step(b, first=False, second=False, last=False):
                more = not last
                take_qk(b)
                scale_heads(b, 0)
                take_v(b, (0, 1))
                v_hi(b, (0, 1))
                if not first:
                    make_y(b - 1, 0)
                    make_y(b - 1, 1)
                scale_heads(b, 1)
                if first:
                    split_hi("o", w_o, raw_o)
                    sc.wait_ge(s_stage["w1"], 16 * DC)
                    for c in range(DC):
                        sc.activation(w_1[0][:, c:c + 1, :], raw_1[c], ACT.Copy).then_inc(s_whi, 1)
                take_v(b, (2, 3))
                take_gate(b, 0)
                v_hi(b, (2, 3))
                take_gate(b, 1)
                if not first:
                    y_hi(b - 1, 0)
                take_gate(b, 2)
                take_lk(b)
                if not first:
                    y_hi(b - 1, 1)
                take_gate(b, 3)
                if more:
                    rows_hi(b + 1, 0)
                lq_hi(b)
                take_kv(b)
                if not first:
                    switch_table(ACT.Gelu_apprx_tanh)
                if more:
                    rows_hi(b + 1, 1)
                if not first:
                    take_ys(b - 1)
                gated_hi(b, 0)
                if more:
                    rows_hi(b + 1, 2)
                    take_h(b + 1, 0)
                gated_hi(b, 1)
                if not first:
                    router_tanh(b - 1)
                    gelu(b - 1, 0)
                    gelu(b - 1, 1)
                if more:
                    rows_hi(b + 1, 3)
                gated_hi(b, 2)
                if not first:
                    gelu(b - 1, 2)
                if more and not first:
                    take_h(b + 1, 1)
                gated_hi(b, 3)
                if first:
                    take_h(b + 1, 1)
                if first:
                    sc.wait_ge(s_stage["w2"], 16 * 2)
                    for i in range(2):
                        sc.activation(w_2[0][:, bass.ts(i, FC // 2), :], raw_2[i], ACT.Copy).then_inc(s_whi, 1)
                if not first:
                    gelu(b - 1, 3)
                if more:
                    make_z(b + 1, 0)
                if not first:
                    gelu(b - 1, 4)
                    gelu(b - 1, 5)
                if more:
                    zT_hi(b + 1, 0)
                    make_z(b + 1, 1)
                if not first:
                    gelu(b - 1, 6)
                if more:
                    zT_hi(b + 1, 1)
                if not first:
                    gelu(b - 1, 7)
                if more:
                    switch_table(ACT.Silu)
                if not first:
                    upd_hi(b - 1)

            step(0, first=True)
            step(1, second=True)
            with sc.Fori(2, BATCHES - 1) as b:
                step(b)
            step(BATCHES - 1, last=True)
            make_y(BATCHES - 1, 0)
            make_y(BATCHES - 1, 1)
            y_hi(BATCHES - 1, 0)
            y_hi(BATCHES - 1, 1)
            router_tanh(BATCHES - 1)
            take_ys(BATCHES - 1)
            for f in range(FC):
                gelu(BATCHES - 1, f)
            upd_hi(BATCHES - 1)

        @block.vector
        def _(ve):
            ve.memset(ids[:, BATCHES * TILES:], VOCAB).then_inc(s_set, 1)
            ve.wait_ge(s_ids, 16)
            ve.tensor_scalar(ids[:, 0:BATCHES * TILES], ids[:, 0:BATCHES * TILES].bitcast(mybir.dt.uint32),
                             float(VOCAB), None, ALU.min).then_inc(s_cast, 1)
            for rows_ in (bv_rows, bo_rows, b2_rows):
                ve.memset(f32(rows_[:, :]), 0.0).then_inc(s_set, 1)
            ve.memset(f32(ones[:, :]), 1.0).then_inc(s_set, 1)
            ve.memset(counts[:, :, :], 0.0).then_inc(s_set, 1)

            def split_lo(k, w, raw):
                ve.wait_ge(s_whi, SPLIT[k])
                ve.tensor_tensor(w[1][:, :, :], raw, f32(w[0][:, :, :]), ALU.subtract).then_inc(s_wlo, 1)

            def split_half_lo(k, i, w, raw):
                ve.wait_ge(s_whi, SPLIT[k] - 1 + i)
                ve.tensor_tensor(w[1], raw, f32(w[0]), ALU.subtract).then_inc(s_wlo, 1)

            def split_row(rows_, raw, before_):
                ve.tensor_copy(rows_[0:1, :], raw).then_inc(s_bias, 1)
                ve.wait_ge(s_bias, before_ + 1)
                ve.tensor_tensor(rows_[32:33, :], raw, f32(rows_[0:1, :]), ALU.subtract).then_inc(s_bias, 1)

            def scale_weight(k, raw):
                ve.wait_ge(s_raw_used, 1 + ("qk", "g", "v").index(k))
                for c in range(DC):
                    ve.tensor_scalar(raw[:, c, :], raw[:, c, :], ln1_w[:, c:c + 1], None, ALU.mult).then_inc(s_scaled, 1)

            def normal_stats(i, b, p, x):
                for t in (2 * p, 2 * p + 1):
                    done(ve.bn_stats(stats[i][:, t, :], x(t)), f"stat{i}")
                after_apart(ve, (f"stat{i}", b, 2 * p + 1))
                for t in (2 * p, 2 * p + 1):
                    done(ve.bn_aggr(mv[i][:, t, :], stats[i][:, t, :]), f"mv{i}")

            def root_arg(i, b, scale, add):
                after(ve, f"mv{i}", b)
                after(ve, f"rstd{i}", b - 1)
                if i != 1:
                    after(ve, f"shift{i}", b - 1)
                    ve.tensor_scalar(neg_mean[i][:, :], mv[i][:, :, 0], -1.0, None, ALU.mult)
                done(ve.tensor_scalar(arg[i][:, :], mv[i][:, :, 1], scale, add, ALU.mult, ALU.add), f"arg{i}")

            def rows_lo(b, t):
                after(ve, "rows_hi", b, t)
                done(ve.tensor_tensor(rowsT[1][:, t % 2, :], ps[:, 0, 0:EC * P], f32(rowsT[0][:, t % 2, :]),
                                      ALU.subtract), "rows_lo")

            def h_stats(b, p):
                after(ve, "h", b, p)
                normal_stats(0, b, p, lambda t: h[:, t, :])
                if p == 1:
                    root_arg(0, b, 1.0 + EPS, EPS * EPS)

            def zT_lo(b, p):
                after(ve, "zT_hi", b, p)
                o = zT[1][:, :, D * p:D * p + D].rearrange("p c (t x) -> p t c x", x=P)
                hi = f32(zT[0][:, :, D * p:D * p + D]).rearrange("p c (t x) -> p t c x", x=P)
                done(ve.tensor_tensor(o, ps[:, p, :].rearrange("p (t c x) -> p t c x", t=2, c=DC), hi,
                                      ALU.subtract), "zT_lo")

            def rope(b, p):
                after(ve, "scaled", b, 2 * p)
                after(ve, "quad_ps", b - 1)
                after(ve, "lkT_ps", b - 1)
                done(ve.tensor_tensor(heads[:, p, :], scaled[:, 0, :], cos, ALU.mult), "rope")
                after(ve, "scaled", b, 2 * p + 1)
                done(ve.tensor_tensor(scaled[:, 1, :], scaled[:, 1, :], sin, ALU.mult), "rope")
                after(ve, "rope", b, 3 * p + 1)
                done(ve.tensor_tensor(heads[:, p, :], heads[:, p, :], scaled[:, 1, :], ALU.add), "rope")

            def split_lq(b):
                after(ve, "lq_hi", b)
                done(ve.tensor_tensor(lq[1][QK:P, :], heads[0:QK, 0, :], f32(lq[0][0:QK, :]), ALU.subtract), "lq_lo")

            def take_rank_row(b):
                after(ve, "rrow_ps", b)
                after(ve, "put_ps", b - 1)
                for k in range(2):
                    done(ve.tensor_scalar(put[:, k, :], ps[:, 4, :], slot_of[:, k:k + 1], None, ALU.is_equal), "put")

            def take_ys(b):
                after(ve, "ys_ps", b)
                done(ve.tensor_copy(ys[1][:, :, :], ps[:, 7, :].rearrange("p (c n) -> p c n", c=DC)), "ys_lo")

            def split_hidden(b, fs):
                for f in fs:
                    after(ve, "hid_hi", b, f)
                    done(ve.tensor_tensor(hid[1][:, f % RING, :], act[:, f % 2, :], f32(hid[0][:, f % RING, :]),
                                          ALU.subtract), "hid_lo")

            def split_update(b):
                after(ve, "upd_hi", b)
                done(ve.tensor_tensor(updp[1][:, :, :], ps[:, 6, :].rearrange("p (k n) -> p k n", k=2), f32(updp[0][:, :, :]), ALU.subtract), "upd_lo")

            def result(b):
                for t in range(TILES):
                    after(ve, "put_ps", b, t // 2)
                    after(ve, "base", b, t)
                    if t == 0 and not (isinstance(b, int) and b == 0):
                        ve.wait_ge(sems["stored"], b * 16)
                    done(ve.scalar_tensor_tensor(ob[:, t, :], ps[:, 5 + 2 * (t // 2), half(t)], weight[:, t:t + 1],
                                                 base[:, t, :], ALU.mult, ALU.add), "res")

            def take_lk(b):
                after(ve, "lk_hi", b)
                done(ve.tensor_tensor(lk[:, :, 1, :], ps[:, 3, 0:TILES * QK].rearrange("p (t c) -> p t c", c=QK),
                                      f32(lk[:, :, 0, :]), ALU.subtract), "lk_lo")

            def take_quad(b):
                after(ve, "quad_ps", b)
                blocks = [slice(GROUP * g, GROUP * g + GROUP) for g in range(2)]
                for g, r in enumerate(blocks):
                    done(ve.scalar_tensor_tensor(
                        pre[r, :, :], ps[r, 2, :].rearrange("p (t x) -> p t x", x=P)[:, :, r], 1.0 / GROUP,
                        rel_bias[r, :].unsqueeze(1).to_broadcast([GROUP, TILES, GROUP]), ALU.mult, ALU.add), "pre")
                after(ve, "out_ps", b - 1)
                for g, r in enumerate(blocks):
                    after(ve, "pre", b, g)
                    done(ve.scalar_tensor_tensor(attnT[r, :, r], pre[r, :, :], 0.0, pre[r, :, :],
                                                 ALU.max, ALU.mult), "attn")

            def split_kv(b):
                after(ve, "kv_hi", b)
                done(ve.tensor_tensor(kv[1][0:QK, :], ps[0:QK, 3, :], f32(kv[0][0:QK, :]), ALU.subtract), "kv_lo")

            def take_out(b, e):
                after(ve, "out_ps", b, e)
                after(ve, "gate", b, e)
                done(ve.tensor_tensor(gate[:, e, :], ps[:, 2 if e % 2 == 0 else 4, :], gate[:, e, :], ALU.mult), "prod")
                after(ve, "gated_hi", b, e)
                done(ve.tensor_tensor(gated[1][:, e, :], gate[:, e, :], f32(gated[0][:, e, :]), ALU.subtract), "gated_lo")

            def wo_stats(b, p):
                after(ve, "wo_ps", b, p)
                normal_stats(1, b, p, lambda t: ps[:, 3 + p, half(t)])
                if p == 1:
                    root_arg(1, b, 1.0, EPS)

            def tail2(b, p, between=None):
                after(ve, "rstd1", b)
                after(ve, "h_plus", b)
                for t in (2 * p, 2 * p + 1):
                    done(ve.scalar_tensor_tensor(x2[:, t, :], ps[:, 3 + p, half(t)], mv[1][:, t, 0:1], ln2w_all,
                                                 ALU.subtract, ALU.mult), "t2")
                for t in (2 * p, 2 * p + 1):
                    after(ve, "t2", b, t)
                    done(ve.scalar_tensor_tensor(x2[:, t, :], x2[:, t, :], rstd[1][:, t:t + 1], h_plus[:, t, :],
                                                 ALU.mult, ALU.add), "h2")
                if between:
                    between()
                after(ve, "h2", b, 2 * p + 1)
                normal_stats(2, b, p, lambda t: x2[:, t, :])
                if p == 1:
                    root_arg(2, b, 1.0, EPS)

            def scores(b, p):
                after(ve, "tanh", b - 1)
                for t in (2 * p, 2 * p + 1):
                    after(ve, "y", b, t)
                    item(ve, "score", b, t - 2)
                    done(ve.tensor_tensor_reduce(junk[:, half(t)], y[:, t, :], router_all, 1.0, 0.0,
                                                 ALU.mult, ALU.add, score[:, t:t + 1]), "score")

            def count_higher(b, ts):
                after(ve, "srow_ps", b)
                for t in ts:
                    s = score[:, t:t + 1]
                    from_t = ps[:, 4, P * t:SEQ]
                    room = [junk8[:, SEQ * i:SEQ * i + SEQ] for i in (t % 2, 2 + t % 2)]
                    if t >= 2:
                        after(ve, "count", b, (1, 4)[t - 2])
                    done(ve.tensor_scalar(room[0][:, P * t:SEQ], from_t, s, 0.0, ALU.is_gt, ALU.add,
                                          accum_out=counts[:, t, 0:1]), "count")
                    if t:
                        done(ve.tensor_scalar(room[0][:, 0:P * t], ps[:, 4, 0:P * t], s, 0.0, ALU.is_ge, ALU.add,
                                              accum_out=counts[:, t, 1:2]), "count")
                    done(ve.scalar_tensor_tensor(room[1][:, 0:P], ps[:, 4, tok(t)], s, before, ALU.is_equal,
                                                 ALU.mult, accum_out=counts[:, t, 2:3]), "count")

            def make_rank(b):
                after(ve, "count", b)
                after(ve, "rrow_ps", b - 1)
                done(ve.tensor_reduce(rank[:, :], counts[:, :, :], AX.X, ALU.add), "rank")

            def make_pick(b):
                after(ve, "rank", b)
                after(ve, "ys_ps", b - 1)
                for t in range(TILES):
                    done(ve.tensor_scalar(pick[:, t, :], slots, rank[:, t:t + 1], None, ALU.is_equal), "pick")

            def make_weight(b):
                after(ve, "tanh", b)
                done(ve.tensor_scalar(weight[:, :], half_tanh[:, :], 0.5, 0.5, ALU.mult, ALU.add), "weight")

            ve.wait_ge(s_early, 16)
            ve.tensor_scalar(head_gain[0:QK, 2:4], head_gain[0:QK, 2:4], 1.0 / SEQ, None, ALU.mult).then_inc(s_set, 1)
            ve.tensor_scalar(head_bias[0:QK, 2:4], head_bias[0:QK, 2:4], 1.0 / SEQ, None, ALU.mult).then_inc(s_set, 1)
            split_lo("proj", w_proj, raw_proj)
            rows_lo(0, 0)
            rows_lo(0, 1)
            h_stats(0, 0)
            scale_weight("qk", raw_qk)
            ve.tensor_tensor(b_qk, b_qk, ps[:, 3, 0:1], ALU.add).then_inc(s_bias, 1)
            split_lo("qk", w_qk, raw_qk)
            rows_lo(0, 2)
            rows_lo(0, 3)
            ve.wait_ge(s_pos, 16)
            mid = GROUP - 1
            far = pos_row[0:1, MAX_REL:MAX_REL + 1]
            ve.tensor_copy(rel_row[0:1, mid:mid + MAX_REL + 1], pos_row[0:1, :]).then_inc(s_rel_row, 1)
            for k in range(1, MAX_REL + 1):
                ve.tensor_copy(rel_row[0:1, mid - k:mid - k + 1], pos_row[0:1, k:k + 1])
            ve.tensor_copy(rel_row[0:1, 0:mid - MAX_REL], far.to_broadcast([1, mid - MAX_REL])).then_inc(s_rel_row, 1)
            ve.tensor_copy(rel_row[0:1, mid + MAX_REL + 1:], far.to_broadcast([1, 2 * GROUP - mid - MAX_REL - 1])
                           ).then_inc(s_rel_row, 1)
            h_stats(0, 1)
            scale_weight("v", raw_v)
            scale_weight("g", raw_g)
            zT_lo(0, 0)
            zT_lo(0, 1)
            ve.tensor_tensor(b_g, b_g, ps[:, 4, 0:HC], ALU.add).then_inc(s_bias, 1)
            ve.wait_ge(s_const, N_CONST)
            ve.tensor_tensor(bv_raw, bv_raw, ps[0:1, 5, :], ALU.add).then_inc(s_bias, 1)
            ve.wait_ge(s_bias, 3)
            ve.wait_ge(s_set, 8)
            split_row(bv_rows, bv_raw, 3)
            split_lo("v", w_v, raw_v)
            split_lo("g", w_g, raw_g)
            ve.wait_ge(s_pool_set, 4)
            ve.wait_ge(s_rel, 16 * 2)

            def step(b, first=False, second=False, last=False):
                more = not last
                rope(b, 0)
                if first:
                    split_row(bo_rows, bo_raw, 5)
                    split_row(b2_rows, b2_raw, 7)
                    split_lo("o", w_o, raw_o)
                if not first and not second:
                    result(b - 2)
                if not first:
                    scores(b - 1, 0)
                    scores(b - 1, 1)
                rope(b, 1)
                if first:
                    for c in range(DC):
                        split_half_lo("w1", c, both(w_1, lambda x: x[:, c:c + 1, :]), raw_1[c])
                if not first:
                    count_higher(b - 1, (0, 1, 2))
                take_lk(b)
                if not first:
                    count_higher(b - 1, (3,))
                    make_rank(b - 1)
                if more:
                    rows_lo(b + 1, 0)
                if not first:
                    make_pick(b - 1)
                take_quad(b)
                split_lq(b)
                split_kv(b)
                if more:
                    rows_lo(b + 1, 1)
                if not first:
                    take_rank_row(b - 1)
                if not first:
                    take_ys(b - 1)
                take_out(b, 0)
                if more:
                    rows_lo(b + 1, 2)
                take_out(b, 1)
                if more:
                    h_stats(b + 1, 0)
                if not first:
                    make_weight(b - 1)
                    split_hidden(b - 1, (0, 1))
                if more:
                    rows_lo(b + 1, 3)
                take_out(b, 2)
                if not first:
                    split_hidden(b - 1, (2,))
                if more and not first:
                    h_stats(b + 1, 1)
                take_out(b, 3)
                if first:
                    h_stats(b + 1, 1)
                if first:
                    for i in range(2):
                        split_half_lo("w2", i, both(w_2, lambda x: x[:, bass.ts(i, FC // 2), :]), raw_2[i])
                if not first:
                    split_hidden(b - 1, (3, 4, 5))
                wo_stats(b, 0)
                if more:
                    zT_lo(b + 1, 0)
                wo_stats(b, 1)
                if not first:
                    split_hidden(b - 1, (6,))
                if more:
                    zT_lo(b + 1, 1)
                if not first:
                    split_hidden(b - 1, (7,))
                tail2(b, 0, None if first else lambda: split_update(b - 1))
                tail2(b, 1)

            step(0, first=True)
            step(1, second=True)
            with ve.Fori(2, BATCHES - 1) as b:
                step(b)
            step(BATCHES - 1, last=True)
            result(BATCHES - 2)
            scores(BATCHES - 1, 0)
            scores(BATCHES - 1, 1)
            count_higher(BATCHES - 1, range(TILES))
            make_rank(BATCHES - 1)
            make_pick(BATCHES - 1)
            make_weight(BATCHES - 1)
            take_rank_row(BATCHES - 1)
            take_ys(BATCHES - 1)
            split_hidden(BATCHES - 1, range(FC))
            split_update(BATCHES - 1)
            result(BATCHES - 1)

        @block.tensor
        def _(pe):
            def bias_products(k):
                pe.wait_ge(s_stage[k], 16)
                if k == "qk":
                    for c in range(DC):
                        m = pe.matmul(ps[:, 3, 0:1], raw_qk[:, c, :], ln1_b[:, c:c + 1], start=(c == 0), stop=(c == 1))
                if k == "g":
                    for e in range(HC):
                        for c in range(DC):
                            m = pe.matmul(ps[:, 4, e:e + 1], raw_g[:, c, tok(e)], ln1_b[:, c:c + 1],
                                          start=(c == 0), stop=(c == 1))
                if k == "v":
                    for c in range(DC):
                        m = pe.matmul(ps[0:1, 5, :], ln1_b[:, c:c + 1], raw_v[:, c, :], start=(c == 0), stop=(c == 1))
                m.then_inc(s_raw_used, 1)

            def rows_T(b, t):
                pe.wait_ge(gathered[t], (b + 1) * 16)
                if t == 0:
                    after(pe, "gate", b - 1, 2)
                else:
                    after(pe, "rows_lo", b, t - 1)
                for c in range(EC):
                    m = pe.transpose(ps[:, 0, tok(c)], rows[:, t, tok(c)], ident)
                done(m, "rowsT_ps")

            def embed_mm(b, t):
                after(pe, "rows_lo", b, t)
                if t == 0:
                    after(pe, "gate", b - 1)
                if t == 2:
                    after(pe, "h", b, 0)
                for c in range(EC):
                    m = mm3(pe, ps[:, 1, half(t)], both(rowsT, lambda x: x[:, t % 2, tok(c)]),
                            both(w_proj, lambda x: x[:, c, :]), c == 0, c == EC - 1)
                if t % 2:
                    done(m, "h_ps")

            def z_T(b, p):
                after(pe, "rows_lo", b)
                after(pe, "h", b)
                for t in (2 * p, 2 * p + 1):
                    after(pe, "z", b, t)
                    for c in range(DC):
                        m = pe.transpose(ps[:, t // 2, D * (t % 2) + P * c:D * (t % 2) + P * c + P],
                                         z[:, t % 2, tok(c)], ident)
                    done(m, "zT_ps")

            def qk(b):
                after(pe, "zT_lo", b)
                for c in range(DC):
                    m = mm3(pe, ps[:, 0, :], both(w_qk, lambda x: x[:, c, :]),
                            both(zT, lambda x: x[:, c, :]), c == 0, c == 1)
                done(m, "qk_ps")

            def vs(b, ts):
                after(pe, "prod", b - 1)
                after(pe, "t2", b - 1, 1)
                for t in ts:
                    if t >= 2:
                        after(pe, "v", b, t - 2)
                    pe.matmul(ps[:, 2 + t % 2, :], ones[:, :], bv_rows[:, :], start=True, stop=False)
                    for c in range(DC):
                        m = mm3(pe, ps[:, 2 + t % 2, :], both(zT, lambda x: x[:, c, tok(t)]),
                                both(w_v, lambda x: x[:, c, :]), False, c == 1)
                    done(m, "v_ps")

            def gates(b, e):
                if e < 2:
                    after(pe, "qk", b)
                else:
                    after(pe, "gate", b, e - 2)
                for c in range(DC):
                    m = mm3(pe, ps[:, e % 2, :], both(w_g, lambda x: x[:, c, tok(e)]),
                            both(zT, lambda x: x[:, c, :]), c == 0, c == 1)
                done(m, "gate_ps")

            def rank_row(b):
                after(pe, "rank", b)
                for t in range(TILES):
                    m = pe.transpose(ps[:, 4, tok(t)], rank[:, t:t + 1].to_broadcast([P, P]), ident)
                done(m, "rrow_ps")

            def select(b):
                after(pe, "pick", b)
                after(pe, "y_lo", b)
                after(pe, "upd_lo", b - 1)
                after(pe, "res", b - 1)
                for c in range(DC):
                    for part in range(2):
                        for t in range(TILES):
                            m = pe.matmul(ps[:, 6 + part, TOP * c:TOP * c + TOP], y_split[part][:, t, tok(c)],
                                          pick[:, t, :], start=(t == 0), stop=(t == TILES - 1))
                done(m, "ys_ps")

            def ff1(b, g):
                if g == 0:
                    after(pe, "ys_hi", b)
                    after(pe, "ys_lo", b)
                if g >= 2:
                    after(pe, "act", b, 2 * g - 3)
                for f in (2 * g, 2 * g + 1):
                    for c in range(DC):
                        m = mm3(pe, ps[:, 5 + 2 * (g % 2), half(f)], both(w_1, lambda x: x[:, c, tok(f)]),
                                both(ys, lambda x: x[:, c, :]), c == 0, c == 1)
                done(m, "ff1_ps")

            def ff2(b, f):
                after(pe, "hid_lo", b, f)
                if f == 0:
                    pe.matmul(ps[:, 6, :], ones[:, :], b2_rows[:, :], start=True, stop=False, skip_group_check=True)
                for k in range(2):
                    for i, j in ((0, 0), (1, 0), (0, 1)):
                        m = pe.matmul(ps[:, 6, half(k)], hid[i][:, f % RING, tok(k)], w_2[j][:, f, :],
                                      start=False, stop=(f == FC - 1 and j == 1),
                                      skip_group_check=True)
                done(m, "ff2_ps")

            def put_back(b):
                after(pe, "upd_lo", b)
                after(pe, "put", b)
                after(pe, "act", b)
                for t in range(TILES):
                    n = 0
                    for k in range(2):
                        for part in range(2):
                            m = pe.matmul(ps[:, 5 + 2 * (t // 2), half(t)], put[:, k, tok(t)], updp[part][:, k, :],
                                          start=(n == 0), stop=(n == 3))
                            n += 1
                    if t % 2:
                        done(m, "put_ps")

            def quad(b):
                after(pe, "rope", b)
                after(pe, "v", b)
                for t in range(TILES):
                    m = pe.matmul(ps[:, 2, tok(t)], heads[QK:P, 1, tok(t)], heads[QK:P, 0, tok(t)],
                                  start=True, stop=True)
                done(m, "quad_ps")
                for t in range(TILES):
                    m = pe.transpose(ps[:, 3, QK * t:QK * t + QK], heads[0:QK, 1, tok(t)], ident[0:QK, 0:QK])
                done(m, "lkT_ps")

            def kvs(b):
                after(pe, "lk_lo", b)
                for t in range(TILES):
                    after(pe, "v_lo", b, t)
                    pe.matmul(ps[:, 3, :], lk[:, t, :, :], v_split[0][:, t, :], start=(t == 0), stop=(t == TILES - 1),
                              skip_group_check=True)
                    m = pe.matmul(ps[0:QK, 3, :], lk[:, t, 0, :], v_split[1][:, t, :], start=False,
                                  stop=(t == TILES - 1), skip_group_check=True)
                    done(m, "kv_ps")

            def outs(b, e):
                bank = 2 if e % 2 == 0 else 4
                if e == 1:
                    after(pe, "put", b - 1)
                if e == 0:
                    after(pe, "kv_lo", b)
                    after(pe, "lq_lo", b)
                    after(pe, "attn", b)
                if e >= 2:
                    after(pe, "prod", b, e - 2)
                for i in range(2):
                    pe.matmul(ps[:, bank, :], kv[i][:, tok(e)], lq[i][:, :], start=(i == 0), stop=False,
                              skip_group_check=True)
                for t in range(TILES):
                    m = pe.matmul(ps[:, bank, tok(t)], v[:, t, tok(e)], attnT[:, t, :],
                                  start=False, stop=True, skip_group_check=True)
                done(m, "out_ps")

            def project(b, p):
                after(pe, "gated_lo", b)
                pe.matmul(ps[:, 3 + p, :], ones[:, :], bo_rows[:, :], start=True, stop=False, skip_group_check=True)
                for t in (2 * p, 2 * p + 1):
                    for e in range(HC):
                        m = mm3(pe, ps[:, 3 + t // 2, half(t)], both(gated, lambda x: x[:, e, tok(t)]),
                                both(w_o, lambda x: x[:, e, :]), False, e == HC - 1, shared=True)
                    if t % 2:
                        done(m, "wo_ps")

            def score_row(b):
                after(pe, "score", b)
                after(pe, "t2", b)
                for t in range(TILES):
                    m = pe.transpose(ps[:, 4, tok(t)], score[:, t:t + 1].to_broadcast([P, P]), ident)
                done(m, "srow_ps")

            pe.wait_ge(s_early, 16)
            pe.wait_ge(s_pool_set, 4)
            rows_T(0, 0)
            pe.wait_ge(s_wlo, SPLIT["proj"])
            embed_mm(0, 0)
            rows_T(0, 1)
            bias_products("qk")
            embed_mm(0, 1)
            rows_T(0, 2)
            bias_products("g")
            embed_mm(0, 2)
            rows_T(0, 3)
            embed_mm(0, 3)
            bias_products("v")
            z_T(0, 0)
            z_T(0, 1)
            pe.wait_ge(s_wlo, SPLIT["qk"])

            def step(b, first=False, second=False, last=False):
                more = not last
                qk(b)
                if first:
                    pe.wait_ge(s_bias, 5)
                    pe.wait_ge(s_set, 8)
                    pe.wait_ge(s_wlo, SPLIT["v"])
                vs(b, (0, 1))
                if not first and not second:
                    put_back(b - 2)
                if first:
                    pe.wait_ge(s_wlo, SPLIT["g"])
                vs(b, (2, 3))
                gates(b, 0)
                gates(b, 1)
                if not first:
                    score_row(b - 1)
                gates(b, 2)
                quad(b)
                gates(b, 3)
                if more:
                    rows_T(b + 1, 0)
                kvs(b)
                if not first:
                    rank_row(b - 1)
                if more:
                    embed_mm(b + 1, 0)
                    rows_T(b + 1, 1)
                if not first:
                    select(b - 1)
                outs(b, 0)
                if more:
                    embed_mm(b + 1, 1)
                    rows_T(b + 1, 2)
                outs(b, 1)
                if second:
                    pe.wait_ge(s_wlo, SPLIT["w2"])
                if not first:
                    ff1(b - 1, 0)
                if more:
                    embed_mm(b + 1, 2)
                    rows_T(b + 1, 3)
                outs(b, 2)
                if not first:
                    ff1(b - 1, 1)
                if more and not first:
                    embed_mm(b + 1, 3)
                outs(b, 3)
                if first:
                    embed_mm(b + 1, 3)
                if not first:
                    ff2(b - 1, 0)
                    ff2(b - 1, 1)
                    ff1(b - 1, 2)
                    ff2(b - 1, 2)
                if first:
                    pe.wait_ge(s_wlo, SPLIT["o"])
                    pe.wait_ge(s_bias, 9)
                project(b, 0)
                if more:
                    z_T(b + 1, 0)
                project(b, 1)
                if not first:
                    ff1(b - 1, 3)
                    ff2(b - 1, 3)
                if more:
                    z_T(b + 1, 1)
                if not first:
                    for f in range(4, FC):
                        ff2(b - 1, f)

            step(0, first=True)
            step(1, second=True)
            with pe.Fori(2, BATCHES - 1) as b:
                step(b)
            step(BATCHES - 1, last=True)
            put_back(BATCHES - 2)
            score_row(BATCHES - 1)
            rank_row(BATCHES - 1)
            select(BATCHES - 1)
            ff1(BATCHES - 1, 0)
            ff1(BATCHES - 1, 1)
            for g in range(FC // 2):
                ff2(BATCHES - 1, 2 * g)
                ff2(BATCHES - 1, 2 * g + 1)
                if g < 2:
                    ff1(BATCHES - 1, g + 2)
            put_back(BATCHES - 1)


def constants():
    half = QK // 2
    inv = (np.float32(10000.0) ** (-np.arange(half, dtype=np.float32) / np.float32(half))).astype(np.float32)
    ang = (np.arange(SEQ, dtype=np.float32)[:, None] * inv[None, :]).astype(np.float32)
    sin, cos = np.sin(ang).T, np.cos(ang).T
    return {
        "cos": np.concatenate([cos] * 4).astype(np.float32),
        "sin": np.concatenate([-sin, sin, sin, -sin]).astype(np.float32),
        "ident": np.eye(P, dtype=np.float32),
        "before": (np.arange(P)[None, :] < np.arange(P)[:, None]).astype(np.float32),
        "slots": np.tile(np.arange(TOP, dtype=np.float32), (P, 1)),
        "slot_of": (np.arange(P)[:, None] + P * np.arange(2)[None, :]).astype(np.float32),
    }


def kernel(**inputs):
    import concourse.bacc as bacc
    from concourse.bass_utils import run_bass_kernel_spmd

    g = {k: np.asarray(x) for k, x in inputs.items()}
    table = np.zeros((VOCAB + 1, ROW), np.float32)
    proj = np.zeros((EC * P, D), np.float32)
    row = col = 0
    for i, w in enumerate(WIDTHS):
        emb = g[f"L0_tok_emb_{i}"]
        table[row:row + emb.shape[0], col:col + w] = emb
        proj[col:col + w] = g[f"L0_tok_proj_{i}"].T
        row, col = row + emb.shape[0], col + w

    def rows_of(w, chunks):
        return np.ascontiguousarray(w.reshape(chunks, P, -1).transpose(1, 0, 2))

    def column(x, n):
        return np.ascontiguousarray(x.reshape(n, P).T)

    def swap(x):
        return np.concatenate([x[QK // 2:], x[:QK // 2]])

    wqk = g["L0_attn_Wqk"]

    def by_head(x):
        q, lq, k, lk = x
        cols = []
        for lin, quad in ((lq, q), (lk, k)):
            cols += [np.concatenate([lin, swap(quad)]), np.concatenate([swap(lin), quad])]
        return np.ascontiguousarray(np.stack(cols, 1))

    bqk = g["L0_attn_bqk"]
    columns = {
        "ln1_w": column(g["L0_attn_ln1_w"], DC),
        "ln1_b": column(g["L0_attn_ln1_b"], DC),
        "b_qk": column(np.concatenate([bqk, swap(bqk)]), 1),
        "b_g": column(g["L0_attn_bg"], HC),
        "b_1": column(g["L0_ffn_b1"], FC),
        "head_gain": by_head(g["L0_attn_gamma"]),
        "head_bias": by_head(g["L0_attn_beta"]),
        **constants(),
    }

    def side_by_side(names):
        return np.ascontiguousarray(np.concatenate([columns[name] for name, _ in names], 1))

    arrays = {
        "ids": np.ascontiguousarray(g["x"].reshape(-1, P).T),
        "table": table,
        "w_proj": rows_of(proj, EC),
        "w_qk": rows_of(np.concatenate([wqk, swap(wqk)]).T, DC),
        "w_v": rows_of(g["L0_attn_Wv"].T, DC),
        "w_g": rows_of(g["L0_attn_Wg"].T, DC),
        "w_o": rows_of(g["L0_attn_Wo"].T, HC),
        "w_w1": rows_of(g["L0_ffn_W1"], DC),
        "w_w2": rows_of(g["L0_ffn_W2"], FC),
        "early": side_by_side(COLUMNS[:-len(LATE)]),
        "late": side_by_side(LATE),
        "b_v": g["L0_attn_bv"].reshape(1, H),
        "b_o": np.tile(g["L0_attn_bo"], 2).reshape(1, 2 * D),
        "b_2": np.tile(g["L0_ffn_b2"], 2).reshape(1, 2 * D),
        "rows": np.concatenate([g["L0_attn_ln2_w"], g["L0_attn_ln2_b"], g["L0_ffn_w_router"].reshape(-1)]),
        "pos": g["L0_attn_pos_emb"][:MAX_REL + 1].reshape(1, -1),
    }
    nc = bacc.Bacc("TRN2", target_bir_lowering=False, num_devices=1)
    aps = {k: nc.dram_tensor("in_" + k, x.shape, mybir.dt.from_np(x.dtype), kind="ExternalInput").ap()
           for k, x in arrays.items()}
    out = nc.dram_tensor("out_0", (BATCHES * SEQ, D), F32, kind="ExternalOutput").ap()
    build(nc, aps, out)
    r = run_bass_kernel_spmd(nc, [{"in_" + k: x for k, x in arrays.items()}], core_ids=[0])
    return r.results[0]["out_0"].reshape(BATCHES, SEQ, D)
```
